# Optimizing a Trainium2 kernel written in Bass

```python
import numpy as np
import jax
import jax.numpy as jnp

def _softmax(x, axis=-1):
    return jax.nn.softmax(x, axis=axis)

def _gelu(x):
    return jax.nn.gelu(x, approximate=True)

def _silu(x):
    return jax.nn.silu(x)

def _sigmoid(x):
    return jax.nn.sigmoid(x)

def _layernorm(x, axis=-1, eps=1e-05):
    m = jnp.mean(x, axis=axis, keepdims=True)
    v = jnp.var(x, axis=axis, keepdims=True)
    return (x - m) / jnp.sqrt(v + eps)

def _scatter_add(tgt, idx, src, axis=0):
    return tgt.at[idx].add(src)

def _segment_sum(src, seg, n):
    return jax.ops.segment_sum(src, seg, n)
kernel_name = 'mk_gnn_resnorm_d1_gnn_r8_f0331b'

def setup_inputs(seed: int=0):
    np.random.seed(seed)
    _w = jnp.asarray

    def _rec_inputs():
        import jax
        import jax.numpy as jnp
        _gk = jax.random.key(seed)
        x = -0.0002117 + 1 * jax.random.normal(jax.random.fold_in(_gk, 1), (6250, 512), jnp.float32)
        _s = jax.random.randint(jax.random.fold_in(_gk, 2), (50000,), 0, 6250, jnp.int32)
        _d = jax.random.randint(jax.random.fold_in(_gk, 3), (50000,), 0, 6250, jnp.int32)
        _loop = jnp.arange(6250, dtype=jnp.int32)
        src = jnp.concatenate([_s, _d, _loop])
        dst = jnp.concatenate([_d, _s, _loop])
        _o = jnp.argsort(dst, stable=True)
        src = src[_o]
        dst = dst[_o]
        return (x, src, dst)
    x, src, dst = _rec_inputs()

    def _L0_gnn_setup():
        import jax, jax.numpy as jnp
        import numpy as np
        N, D = (6250, 512)
        E = 50000
        P_POW, M_SCALE, EPS = (2, 2, 1e-10)

        def _layer_norm(x, gamma, beta, eps=1e-05):
            mu = jnp.mean(x, axis=-1, keepdims=True)
            var = jnp.mean(jnp.square(x - mu), axis=-1, keepdims=True)
            return (x - mu) * jax.lax.rsqrt(var + eps) * gamma + beta

        def _former(Q, V):
            Q = jax.nn.relu(_layer_norm(Q, 1.0, 0.0))
            H = jnp.sum(Q, axis=1, keepdims=True) ** P_POW
            m = (jnp.max(H) - jnp.min(H)) * M_SCALE
            H = jnp.pi / (2.0 * m) * H
            cosQ = Q * jnp.cos(H)
            sinQ = Q * jnp.sin(H)
            out = cosQ @ (cosQ.T @ V) + sinQ @ (sinQ.T @ V)
            norm = cosQ @ jnp.sum(cosQ, axis=0)[:, None] + sinQ @ jnp.sum(sinQ, axis=0)[:, None] + EPS
            return out / norm

        def _gcn(x, edge_index, Wg, bg):
            loop = jnp.arange(N, dtype=edge_index.dtype)
            src = jnp.concatenate([edge_index[0], loop])
            dst = jnp.concatenate([edge_index[1], loop])
            deg = jax.ops.segment_sum(jnp.ones_like(src, dtype=x.dtype), dst, num_segments=N)
            dinv = jax.lax.rsqrt(jnp.maximum(deg, 1e-12))
            coef = (dinv[src] * dinv[dst])[:, None]
            xw = x @ Wg
            return jax.ops.segment_sum(xw[src] * coef, dst, num_segments=N) + bg
        key = jax.random.key(seed)
        ks = jax.random.split(key, 10)
        s = 1.0 / np.sqrt(D)
        return {'x': jax.random.normal(ks[0], (N, D), dtype=jnp.float32), 'edge_index': jax.random.randint(ks[1], (2, E), 0, N, dtype=jnp.int64), 'Wq': jax.random.uniform(ks[2], (D, D), jnp.float32, -s, s), 'bq': jax.random.uniform(ks[3], (D,), jnp.float32, -s, s), 'Wv': jax.random.uniform(ks[4], (D, D), jnp.float32, -s, s), 'bv': jax.random.uniform(ks[5], (D,), jnp.float32, -s, s), 'Wg': jax.random.uniform(ks[6], (D, D), jnp.float32, -s, s), 'bg': jax.random.uniform(ks[7], (D,), jnp.float32, -s, s), 'gamma': jnp.ones((D,), jnp.float32), 'beta': jnp.zeros((D,), jnp.float32)}
    _L0_gnn_all = _L0_gnn_setup()
    _L0_gnn_in = {k: v for k, v in _L0_gnn_all.items() if k in ('Wq', 'bq', 'Wv', 'bv', 'Wg', 'bg', 'gamma', 'beta')}
    del _L0_gnn_all
    return {'x': x, 'src': src, 'dst': dst, 'L0_gnn_Wq': _L0_gnn_in['Wq'], 'L0_gnn_bq': _L0_gnn_in['bq'], 'L0_gnn_Wv': _L0_gnn_in['Wv'], 'L0_gnn_bv': _L0_gnn_in['bv'], 'L0_gnn_Wg': _L0_gnn_in['Wg'], 'L0_gnn_bg': _L0_gnn_in['bg'], 'L0_gnn_gamma': _L0_gnn_in['gamma'], 'L0_gnn_beta': _L0_gnn_in['beta']}

def reference(x, src, dst, L0_gnn_Wq, L0_gnn_bq, L0_gnn_Wv, L0_gnn_bv, L0_gnn_Wg, L0_gnn_bg, L0_gnn_gamma, L0_gnn_beta):
    import jax
    import jax.numpy as jnp

    def _L0_gnn_ref(x, edge_index, Wq, bq, Wv, bv, Wg, bg, gamma, beta):
        import jax, jax.numpy as jnp
        import numpy as np
        N, D = (6250, 512)
        E = 50000
        P_POW, M_SCALE, EPS = (2, 2, 1e-10)

        def _layer_norm(x, gamma, beta, eps=1e-05):
            mu = jnp.mean(x, axis=-1, keepdims=True)
            var = jnp.mean(jnp.square(x - mu), axis=-1, keepdims=True)
            return (x - mu) * jax.lax.rsqrt(var + eps) * gamma + beta

        def _former(Q, V):
            Q = jax.nn.relu(_layer_norm(Q, 1.0, 0.0))
            H = jnp.sum(Q, axis=1, keepdims=True) ** P_POW
            m = (jnp.max(H) - jnp.min(H)) * M_SCALE
            H = jnp.pi / (2.0 * m) * H
            cosQ = Q * jnp.cos(H)
            sinQ = Q * jnp.sin(H)
            out = cosQ @ (cosQ.T @ V) + sinQ @ (sinQ.T @ V)
            norm = cosQ @ jnp.sum(cosQ, axis=0)[:, None] + sinQ @ jnp.sum(sinQ, axis=0)[:, None] + EPS
            return out / norm

        def _gcn(x, edge_index, Wg, bg):
            loop = jnp.arange(N, dtype=edge_index.dtype)
            src = jnp.concatenate([edge_index[0], loop])
            dst = jnp.concatenate([edge_index[1], loop])
            deg = jax.ops.segment_sum(jnp.ones_like(src, dtype=x.dtype), dst, num_segments=N)
            dinv = jax.lax.rsqrt(jnp.maximum(deg, 1e-12))
            coef = (dinv[src] * dinv[dst])[:, None]
            xw = x @ Wg
            return jax.ops.segment_sum(xw[src] * coef, dst, num_segments=N) + bg
        Q = jax.nn.relu(x @ Wq + bq)
        V = x @ Wv + bv
        out = _former(Q, V) + _gcn(x, edge_index, Wg, bg) + V
        out = _layer_norm(out, gamma, beta)
        out = jax.nn.relu(out)
        return out
    edge_index = jnp.stack([src, dst])
    x = _layernorm(x + _L0_gnn_ref(x, edge_index, L0_gnn_Wq, L0_gnn_bq, L0_gnn_Wv, L0_gnn_bv, L0_gnn_Wg, L0_gnn_bg, L0_gnn_gamma, L0_gnn_beta), axis=-1)
    return x

_drawn_inputs = setup_inputs


def setup_inputs(seed=0):
    import zlib

    import numpy as np

    out = dict(_drawn_inputs(seed))
    spreads = {'L0_gnn_gamma': (1.0, 0.2), 'L0_gnn_beta': (0.0, 0.1)}
    factors = {}
    for name, (base, spread) in spreads.items():
        noise = np.random.default_rng([zlib.crc32(name.encode()), seed]).standard_normal(out[name].shape)
        drawn = base * np.exp(spread * noise) if base else spread * noise
        out[name] = jnp.asarray(drawn.astype(out[name].dtype))
    for name, factor in factors.items():
        out[name] = (out[name] * factor).astype(out[name].dtype)
    return out
```

```python
from contextlib import ExitStack

import numpy as np
import concourse.bass as bass
from concourse import mybir

F32 = mybir.dt.float32
F32R = mybir.dt.float32r
BF16 = mybir.dt.bfloat16
I32 = mybir.dt.int32
U32 = mybir.dt.uint32
U16 = mybir.dt.uint16
ALU = mybir.AluOpType
ACT = mybir.ActivationFunctionType
AX = mybir.AxisListType

P = 128
LEAD = 6
BIG = 4096.0
PI = float(np.pi)
TURN_HI = 6.28125
TURN_MID = float(np.float32(2 * np.pi - 6.28125))
TURN_LO = float(2 * np.pi - 6.28125 - TURN_MID)
ROUND = 12582912.0
HALF_PI = float(np.float32(np.pi / 2))


def done(n):
    return n + (1 + LEAD)


def freed(n, depth):
    return n + (1 + LEAD - depth)


def build_layer(nc, x, src, dst, Wq, bq, Wv, bv, Wg, bg, gamma, beta, out):
    N, D = x.shape
    E = src.shape[0]
    B = D // P
    TILES = -(-N // P)
    FULL = N // P
    TAIL = N - FULL * P
    CHUNKS = -(-E // P)
    GROUPS = -(-CHUNKS // P)
    HIST = -(-CHUNKS // TILES)
    PER_TILE = 18
    RING = 6
    SPLIT = 3
    COLS = GROUPS * P
    LN_EPS = 1e-5
    NORM_EPS = 1e-10
    QV_STEPS, COS_STEPS, SIN_STEPS, OUT_STEPS = 3, 4, 6, 4
    QV_LOOPS, COS_LOOPS, SIN_LOOPS = FULL // 3, FULL // 4, FULL // 6
    OUT_LOOPS = FULL // 4 - 1
    COS_SEQ = QV_LOOPS + 1
    SIN_SEQ = COS_SEQ + COS_LOOPS
    OUT_SEQ = SIN_SEQ + SIN_LOOPS
    assert B == 4 and TAIL and FULL == 48 and OUT_SEQ + 1 + OUT_LOOPS == TILES
    assert HIST * TILES <= COLS and CHUNKS + PER_TILE <= COLS and 2 * RING // SPLIT == 4

    table = nc.dram_tensor("scaled_g", [N, D], F32).ap()
    values = nc.dram_tensor("values", [N, D], F32).ap()
    combined = nc.dram_tensor("gcn_plus_values", [N, D], F32).ap()

    ctx = ExitStack()
    with ctx:
        def sb(name, shape, dt):
            return ctx.enter_context(nc.sbuf_tensor(name, shape, dt))

        def sem(name):
            return ctx.enter_context(nc.semaphore(name))

        def bank(name):
            return ctx.enter_context(nc.psum_tensor(name, [P, D], F32))

        nodes = sb("nodes", [P, TILES * D], F32)
        weights = sb("weights", [P, 4, B, D], F32R)
        split = sb("split", [P, 8, D], F32R)
        rows = sb("rows", [P, RING * D], F32)
        operands = sb("operands", [P, 8, D], F32R)
        stage = sb("stage", [P, 6, D], F32)
        own_rows = sb("own_rows", [P, D], F32)
        combine = sb("combine", [P, D], F32)
        bias = sb("bias", [P, 2, D], F32)
        src_cols = sb("src_cols", [P, COLS], U16)
        dst_cols = sb("dst_cols", [P, COLS], F32)
        index_slots = sb("index_slots", [P, RING], U32)
        one_hot = sb("one_hot", [P, SPLIT, P], F32R)
        ident = sb("ident", [P, P], F32)
        ident_r = sb("ident_r", [P, P], F32R)
        node_id = sb("node_id", [P, P], F32)
        tile_id = sb("tile_id", [P, P], F32)
        zeros_r = sb("zeros_r", [P, 8], F32R)
        dinv = sb("dinv", [P, TILES], F32)
        cos_sin = sb("cos_sin", [P, 2 * TILES], F32)
        row_sum = sb("row_sum", [P, TILES], F32)
        schedule = sb("schedule", [1, 2 * TILES], I32)
        stats = sb("stats", [P, 6, 8], F32)
        moment_sums = sb("moment_sums", [P, 8], F32)
        sums_hi = sb("sums_hi", [P, 8], F32R)
        sums_lo = sb("sums_lo", [P, 8], F32R)
        cs_hi = sb("cs_hi", [P, 2 * TILES], F32R)
        cs_lo = sb("cs_lo", [P, 2 * TILES], F32R)
        bn_parts = sb("bn_parts", [P, 3, 6], F32)
        small = sb("small", [P, 16], F32)
        first_node = sb("first_node", [P, TILES], F32)
        ones = sb("ones", [1, P], F32)

        banks = [bank(f"bank{n}") for n in range(8)]
        gcn_bank = banks[0]

        scratch = nodes[:, 0:16 * COLS]
        part = lambda n, w=COLS: nodes[:, n * COLS:n * COLS + w]
        dst_nat = part(0).bitcast(I32)
        src_nat = part(1).bitcast(I32)
        dst_f = part(2)
        src_f = part(3)
        dst_i = part(4).bitcast(I32)
        mod_i = part(5).bitcast(I32)
        div_i = part(6).bitcast(I32)
        neg = part(7)
        bias_raw = part(8, D)
        bins = stage[:, 2, :]
        chunk_id = nodes[:, 9 * COLS:9 * COLS + GROUPS]
        limit = nodes[:, 10 * COLS:10 * COLS + TILES]
        grid = nodes[:, 11 * COLS:11 * COLS + TILES * GROUPS].rearrange("p (t g) -> p t g", g=GROUPS)
        ext = nodes[:, 12 * COLS:12 * COLS + 2 * GROUPS]
        lim_lo = nodes[:, 13 * COLS:13 * COLS + TILES]
        lim_hi = nodes[:, 13 * COLS + 64:13 * COLS + 64 + TILES]
        col = nodes[:, 14 * COLS:14 * COLS + 8]
        dst_mod = combine[:, :].bitcast(BF16)[:, 0:COLS]
        dst_div = own_rows[:, :].bitcast(BF16)[:, 0:COLS]
        HALF = (-(-HIST // 2), HIST // 2)
        mod_hot = [stage[:, 2:6, :].rearrange("p a d -> p (a d)")[:, h * HALF[0] * 64:(h + 1) * HALF[0] * 64]
                   .bitcast(BF16).rearrange("p (c j) -> p c j", j=P) for h in range(2)]
        DIVW = TILES + 1
        div_base = 2 * HALF[0] * 64
        div_hot = [stage[:, 2:6, :].rearrange("p a d -> p (a d)")
                   [:, div_base + h * HALF[0] * DIVW // 2:div_base + (h + 1) * HALF[0] * DIVW // 2]
                   .bitcast(BF16).rearrange("p (c j) -> p c j", j=DIVW) for h in range(2)]
        iota_bf = sb("iota_bf", [P, P], BF16)
        zero_bf = sb("zero_bf", [P, P], BF16)

        raw = rows[:, 0:B * D].rearrange("p (k n) -> p k n", n=D)
        g_hi, g_lo = split[:, 0:4, :], split[:, 4:8, :]
        hi_ring = [split[:, n, :] for n in range(SPLIT)]
        lo_ring = [split[:, SPLIT + n, :] for n in range(SPLIT)]
        own_hi, own_lo = split[:, 6, :], split[:, 7, :]
        row_ring = [rows[:, n * D:(n + 1) * D] for n in range(RING)]

        def plain(ap):
            return ap.bitcast(F32)

        def tile_of(ap, t, w=D):
            return ap[:, t * w:(t + 1) * w] if isinstance(t, int) else ap[:, bass.ds(t * w, w)]

        def dram_rows(ap, t, r):
            return ap[t * P:t * P + r, :] if isinstance(t, int) else ap[bass.ds(t * P, r), :]

        def column(ap, c):
            return ap[:, c:c + 1] if isinstance(c, int) else ap[:, bass.ds(c, 1)]

        s = {}
        for name in (
            "pads_set", "dst_loaded", "src_loaded", "g_raw_loaded", "bias_loaded", "raw_split",
            "q_raw_loaded", "v_raw_loaded", "g_x_turned", "g_scaled", "table_written", "own_split",
            "own_loaded", "combined_stored", "combine_loaded", "qv_x_turned", "m_split", "v_kept",
            "q_biased", "rows_bias_loaded", "moment_split", "consts_set", "chunk_indexed",
            "extra_indexed", "setup_done", "chunk_split", "extra_landed", "extra_summed",
            "raw_rounded", "g_summed", "g_x_hi", "g_kept", "degrees_kept", "root_taken",
            "chunk_summed", "chunk_rounded", "gcn_summed", "own_rounded", "extra_rounded",
            "gcn_combined", "q_summed", "qv_x_hi", "q_rect", "q_stats", "q_root", "q_scaled",
            "q_kept", "angle_ready", "cos_sin_ready", "m_summed", "m_hi", "moment_ready",
            "moment_hi", "cs_rounded", "o_turned", "o_products", "o_hi", "o_norm_ready", "o_first",
            "o_final", "o_scaled2", "dve_chain", "edges_f", "ident_ready", "edges_turned",
            "edges_kept", "limits_ready", "limits_turned", "ranges_ready", "ranges_turned",
            "schedule_ready", "bins_used", "bins_ready", "g_x_split", "degrees_summed",
            "dinv_ready", "chunk_hot", "tile_id_ready", "extra_split", "qv_x_split", "v_summed",
            "spread_step", "extremes_turned", "factor_spread", "cs_split", "o_split", "o_normed",
            "o_mixed", "o_stats1", "o_root1", "o_stats2", "o_root2", "x",
        ):
            s[name] = sem(name)
        landed = [sem(f"row_landed{n}") for n in range(RING)]
        g_x_loaded = [sem(f"g_x_loaded{n}") for n in range(2)]
        x_loaded = [sem(f"x_loaded{n}") for n in range(3)]
        v_stored = [sem(f"v_stored{n}") for n in range(3)]
        mv_loaded = [sem(f"mv_loaded{n}") for n in range(2)]
        ox_loaded = [sem(f"ox_loaded{n}") for n in range(2)]
        oc_loaded = [sem(f"oc_loaded{n}") for n in range(2)]
        oq_loaded = [sem(f"oq_loaded{n}") for n in range(4)]
        o_stored = [sem(f"o_stored{n}") for n in range(2)]

        block = ctx.enter_context(nc.Block())

        def wait_apart(eng, semaphore, value):
            value = eng.to_reg(value) if not isinstance(value, int) else value
            eng.wait_ge(s["setup_done"], 1)
            eng.wait_ge(semaphore, value)

        def chunk_number(seq, k):
            return seq * PER_TILE + k

        @block.sync
        def _(sp):
            sp.wait_ge(s["pads_set"], 1)
            for ap, nat, arrived in ((dst, dst_nat, s["dst_loaded"]), (src, src_nat, s["src_loaded"])):
                view = nat.rearrange("p (g e) -> p g e", e=P)
                whole = (GROUPS - 1) * P
                left = E // P - whole
                sp.dma_start(view[:, 0:GROUPS - 1, :],
                             ap[0:whole * P].rearrange("(g p e) -> p g e", p=P, e=P)).then_inc(arrived, 16)
                sp.dma_start(view[0:left, GROUPS - 1, :],
                             ap[whole * P:(whole + left) * P].rearrange("(p e) -> p e", e=P)).then_inc(arrived, 16)
                sp.dma_start(view[left:left + 1, GROUPS - 1, 0:E - E // P * P],
                             ap[E // P * P:E].rearrange("(p e) -> p e", p=1)).then_inc(arrived, 16)
            sp.dma_start(raw, Wg.rearrange("(k p) n -> p k n", p=P)).then_inc(s["g_raw_loaded"], 16)
            row = lambda v: v.rearrange("(a n) -> a n", a=1).to_broadcast([P, D])
            sp.dma_start(bias[:, 0, :], row(bq)).then_inc(s["bias_loaded"], 16)
            sp.dma_start(bias[:, 1, :], row(bv)).then_inc(s["bias_loaded"], 16)
            sp.dma_start(bias_raw, row(bg)).then_inc(s["bias_loaded"], 16)
            sp.wait_ge(s["raw_split"], 1)
            sp.dma_start(raw, Wq.rearrange("(k p) n -> p k n", p=P)).then_inc(s["q_raw_loaded"], 16)
            sp.wait_ge(s["raw_split"], 2)
            sp.dma_start(raw, Wv.rearrange("(k p) n -> p k n", p=P)).then_inc(s["v_raw_loaded"], 16)

            def g_load(n, t, r):
                sp.wait_ge(s["g_x_turned"], freed(t, 2))
                sp.dma_start(stage[0:r, n, :], dram_rows(x, t, r)).then_inc(g_x_loaded[n], 16)

            with sp.Fori(0, FULL // 2) as i:
                g_load(0, i * 2, P)
                g_load(1, i * 2 + 1, P)
            g_load(0, FULL, TAIL)

            with sp.Fori(0, FULL) as t:
                sp.wait_ge(s["g_scaled"], t + 1)
                sp.dma_start(dram_rows(table, t, P), tile_of(nodes, t)).then_inc(s["table_written"], 16)
            sp.wait_ge(s["g_scaled"], TILES)
            sp.dma_start(dram_rows(table, FULL, TAIL), tile_of(nodes, FULL)[0:TAIL, :])\
                .then_inc(s["table_written"], 16)
            sp.wait_ge(s["table_written"], 16 * TILES)

            def own_load(seq, t, r):
                sp.wait_ge(s["own_split"], freed(seq, 1))
                sp.dma_start(own_rows[0:r, :], dram_rows(table, t, r)).then_inc(s["own_loaded"], 16)

            def combine_load(seq, t, r):
                sp.wait_ge(s["combined_stored"], seq * 16)
                sp.dma_start(combine[0:r, :], dram_rows(values, t, r)).then_inc(s["combine_loaded"], 16)

            def x_load(n, t, r):
                sp.wait_ge(s["qv_x_turned"], freed(t, QV_STEPS))
                sp.dma_start(stage[0:r, n, :], dram_rows(x, t, r)).then_inc(x_loaded[n], 16)

            with sp.Fori(0, QV_LOOPS) as i:
                own_load(i, i, P)
                for j in range(QV_STEPS):
                    x_load(j, i * QV_STEPS + j, P)
                sp.wait_ge(v_stored[0], i * 16 + 16)
                sp.wait_ge(v_stored[1], i * 16)
                sp.wait_ge(v_stored[2], i * 16)
                combine_load(i, i, P)
            own_load(QV_LOOPS, FULL, TAIL)
            x_load(0, FULL, TAIL)
            sp.wait_ge(v_stored[0], 16 * (QV_LOOPS + 1))
            sp.wait_ge(v_stored[1], 16 * QV_LOOPS)
            sp.wait_ge(v_stored[2], 16 * QV_LOOPS)
            combine_load(QV_LOOPS, FULL, TAIL)

            def v_load(sweep, n, slot, t, r):
                sp.wait_ge(s["m_split"], freed(n + sweep * TILES, 2))
                sp.dma_start(stage[0:r, slot, :], dram_rows(values, t, r)).then_inc(mv_loaded[slot], 16)

            sp.wait_ge(s["v_kept"], done(TILES - 1))
            sp.wait_ge(s["q_biased"], done(TILES - 1))
            sp.dma_start(bias[:, 1, :], row(bg)).then_inc(s["rows_bias_loaded"], 16)
            sp.dma_start(bias[:, 0, :], row(gamma)).then_inc(s["rows_bias_loaded"], 16)
            v_load(0, 0, 1, FULL, TAIL)
            with sp.Fori(0, COS_LOOPS) as i:
                own_load(i + COS_SEQ, i + (COS_SEQ - 1), P)
                combine_load(i + COS_SEQ, i + (COS_SEQ - 1), P)
                for j in range(COS_STEPS):
                    v_load(0, i * COS_STEPS + (1 + j), j % 2, i * COS_STEPS + j, P)
            v_load(1, 0, 0, FULL, TAIL)
            with sp.Fori(0, SIN_LOOPS) as i:
                own_load(i + SIN_SEQ, i + (SIN_SEQ - 1), P)
                combine_load(i + SIN_SEQ, i + (SIN_SEQ - 1), P)
                for j in range(SIN_STEPS):
                    v_load(1, i * SIN_STEPS + (1 + j), (1 + j) % 2, i * SIN_STEPS + j, P)

            sp.wait_ge(s["moment_split"], 8)
            sp.dma_start(bias[:, 1, :], row(beta)).then_inc(s["rows_bias_loaded"], 16)

            def f_load(n, slot, t, r):
                sp.wait_ge(s["o_turned"], freed(n, 4))
                sp.dma_start(plain(operands[0:r, 4 + slot, :]), tile_of(nodes, t)[0:r, :])\
                    .then_inc(oq_loaded[slot], 16)

            def out_loads(n, round_, slot, t, r, combined_tiles):
                sp.wait_ge(o_stored[slot], round_ * 16)
                sp.dma_start(stage[0:r, slot, :], dram_rows(x, t, r)).then_inc(ox_loaded[slot], 16)
                if combined_tiles is not None:
                    sp.wait_ge(s["combined_stored"], combined_tiles * 16)
                sp.dma_start(stage[0:r, 2 + slot, :], dram_rows(combined, t, r)).then_inc(oc_loaded[slot], 16)

            own_load(OUT_SEQ, OUT_SEQ - 1, P)
            combine_load(OUT_SEQ, OUT_SEQ - 1, P)
            f_load(0, 0, FULL, TAIL)
            out_loads(0, 0, 0, FULL, TAIL, OUT_SEQ)
            with sp.Fori(0, OUT_LOOPS) as i:
                own_load(i + (OUT_SEQ + 1), i + OUT_SEQ, P)
                for j in range(OUT_STEPS):
                    f_load(i * 4 + (1 + j), (1 + j) % 4, i * 4 + j, P)
                combine_load(i + (OUT_SEQ + 1), i + OUT_SEQ, P)
                for j in range(OUT_STEPS):
                    out_loads(i * 4 + (1 + j), i * 2 + (1 + j) // 2, (1 + j) % 2, i * 4 + j, P, i + (OUT_SEQ + 1))
            for j in range(OUT_STEPS):
                f_load(OUT_LOOPS * 4 + 1 + j, (1 + j) % 4, OUT_LOOPS * 4 + j, P)
            for j in range(OUT_STEPS):
                out_loads(OUT_LOOPS * 4 + 1 + j, OUT_LOOPS * 2 + (1 + j) // 2, (1 + j) % 2, OUT_LOOPS * 4 + j, P,
                          TILES)
            sp.wait_ge(o_stored[0], 16 * (OUT_LOOPS * 2 + 3))
            sp.wait_ge(o_stored[1], 16 * (OUT_LOOPS * 2 + 2))

        @block.gpsimd
        def _(pool):
            pool.memset(dst_nat, -1)
            pool.memset(src_nat, 0).then_inc(s["pads_set"], 1)
            pool.memset(ident[:, :], 0.0).then_inc(s["consts_set"], 1)
            pool.wait_ge(s["consts_set"], 1)
            pool.affine_select(out=ident[:, :], in_=ident[:, :], compare_op=ALU.not_equal, fill=1.0, base=0,
                               pattern=[[-1, P]], channel_multiplier=1).then_inc(s["consts_set"], 1)
            pool.iota(node_id[:, :], pattern=[[1, P]], base=0, channel_multiplier=0,
                      allow_small_or_imprecise_dtypes=True)
            pool.iota(iota_bf[:, :], pattern=[[1, P]], base=0, channel_multiplier=0,
                      allow_small_or_imprecise_dtypes=True)
            pool.iota(chunk_id, pattern=[[P, GROUPS]], base=0, channel_multiplier=1,
                      allow_small_or_imprecise_dtypes=True)
            pool.iota(first_node[:, :], pattern=[[P, TILES]], base=0, channel_multiplier=0,
                      allow_small_or_imprecise_dtypes=True)
            pool.memset(zero_bf[:, :], 0.0).then_inc(s["consts_set"], 1)
            pool.sem_inc(s["chunk_indexed"], LEAD)
            pool.sem_inc(s["extra_indexed"], LEAD)

            pool.wait_ge(s["setup_done"], 1)
            pool.wait_ge(s["table_written"], 16 * TILES)
            extras_done = pool.alloc_register("pool_extras")
            pool.reg_mov(extras_done, 0)

            def gather_tile(seq, t):
                first = pool.value_load(column(schedule, t), min_val=0, max_val=CHUNKS - 1)
                for k in range(0, PER_TILE, 3):
                    slot = k % RING
                    wait_apart(pool, s["chunk_split"], freed(chunk_number(seq, k + 2), RING))
                    pool.tensor_copy(index_slots[:, slot:slot + 3], src_cols[:, bass.ds(first + k, 3)])\
                        .then_inc(s["chunk_indexed"], 1)
                    for n in range(3):
                        if n == 0:
                            wait_apart(pool, s["chunk_indexed"], done(seq * (PER_TILE // 3) + k // 3))
                        pool.indirect_dma_start(
                            out=row_ring[slot + n], out_offset=None, in_=table,
                            in_offset=bass.IndirectOffsetOnAxis(ap=index_slots[:, slot + n:slot + n + 1], axis=0)
                        ).then_inc(landed[slot + n], 16)
                end = pool.value_load(column(schedule, t + TILES), min_val=PER_TILE, max_val=CHUNKS - 1 + PER_TILE)
                with pool.If(end > first + PER_TILE):
                    wait_apart(pool, s["chunk_split"], done(chunk_number(seq, PER_TILE - 1)))
                    with pool.Fori(first + PER_TILE, end) as c:
                        had = pool.snap(extras_done)
                        pool.tensor_copy(index_slots[:, 0:1], column(src_cols, c))\
                            .then_inc(s["extra_indexed"], 1)
                        wait_apart(pool, s["extra_indexed"], had + (1 + LEAD))
                        pool.indirect_dma_start(
                            out=row_ring[0], out_offset=None, in_=table,
                            in_offset=bass.IndirectOffsetOnAxis(ap=index_slots[:, 0:1], axis=0)
                        ).then_inc(s["extra_landed"], 16)
                        pool.wait_ge(s["extra_summed"], had + 1)
                        pool.reg_add(extras_done, extras_done, 1)

            with pool.Fori(0, QV_LOOPS) as i:
                gather_tile(i, i)
            gather_tile(QV_LOOPS, FULL)
            with pool.Fori(COS_SEQ, TILES) as seq:
                gather_tile(seq, seq - 1)

        @block.scalar
        def _(act):
            for name in ("g_x_hi", "g_kept", "chunk_rounded", "own_rounded", "qv_x_hi", "q_rect", "q_root",
                         "q_kept", "m_hi", "o_hi", "o_first", "o_root1", "o_root2", "o_scaled2"):
                act.sem_inc(s[name], LEAD)
            extras_done = act.alloc_register("act_extras")
            act.reg_mov(extras_done, 0)

            for n, (name, hi) in enumerate((("g_raw_loaded", g_hi), ("q_raw_loaded", weights[:, 0, :, :]),
                                            ("v_raw_loaded", weights[:, 2, :, :]))):
                act.wait_ge(s[name], 16)
                act.copy(hi, raw).then_inc(s["raw_rounded"], 1)

            def g_step(t, n, r):
                turned = banks[1 + n][:, :].rearrange("p (b c) -> p b c", c=P)[:, :, 0:r]
                x_hi = operands[:, n, :].rearrange("p (b c) -> p b c", c=P)[:, :, 0:r]
                act.wait_ge(s["g_x_turned"], done(t))
                act.wait_ge(s["g_summed"], freed(t, 2))
                act.copy(x_hi, turned).then_inc(s["g_x_hi"], 1)

            def g_keep(t, n, r):
                act.wait_ge(s["g_summed"], done(t))
                act.copy(tile_of(nodes, t)[0:r, :], banks[3 + n][0:r, :]).then_inc(s["g_kept"], 1)

            act.wait_ge(s["setup_done"], 1)
            with act.Fori(0, FULL // 2) as i:
                g_step(i * 2, 0, P)
                g_step(i * 2 + 1, 1, P)
                g_keep(i * 2, 0, P)
                g_keep(i * 2 + 1, 1, P)
            g_step(FULL, 0, TAIL)
            g_keep(FULL, 0, TAIL)
            act.wait_ge(s["degrees_kept"], 1)
            act.activation(dinv[:, :], dinv[:, :], ACT.Sqrt).then_inc(s["root_taken"], 1)

            def chunk(seq, k):
                n = chunk_number(seq, k)
                act.wait_ge(landed[k % RING], seq * (16 * PER_TILE // RING) + 16 * (k // RING + 1))
                act.wait_ge(s["chunk_summed"], freed(n, SPLIT))
                act.copy(hi_ring[k % SPLIT], row_ring[k % RING]).then_inc(s["chunk_rounded"], 1)

            def own_chunk(seq, r):
                act.wait_ge(s["own_loaded"], seq * 16 + 16)
                act.wait_ge(s["gcn_summed"], freed(seq, 1))
                act.copy(own_hi[0:r, :], own_rows[0:r, :]).then_inc(s["own_rounded"], 1)

            def extra_chunks(seq, t):
                first = act.value_load(column(schedule, t), min_val=0, max_val=CHUNKS - 1)
                end = act.value_load(column(schedule, t + TILES), min_val=PER_TILE, max_val=CHUNKS - 1 + PER_TILE)
                with act.If(end > first + PER_TILE):
                    wait_apart(act, s["chunk_summed"], done(chunk_number(seq, PER_TILE - 1)))
                    with act.Fori(first + PER_TILE, end):
                        had = act.snap(extras_done)
                        act.wait_ge(s["extra_landed"], had * 16 + 16)
                        act.copy(hi_ring[0], row_ring[0]).then_inc(s["extra_rounded"], 1)
                        act.wait_ge(s["extra_summed"], had + 1)
                        act.reg_add(extras_done, extras_done, 1)

            def store_combined(seq, t, r):
                act.wait_ge(s["gcn_combined"], done(seq))
                act.dma_start(dram_rows(combined, t, r), combine[0:r, :]).then_inc(s["combined_stored"], 16)

            def x_round(t, j, r):
                turned = banks[1][:, :].rearrange("p (b c) -> p b c", c=P)[:, :, 0:r]
                x_hi = operands[:, j, :].rearrange("p (b c) -> p b c", c=P)[:, :, 0:r]
                act.wait_ge(s["qv_x_turned"], done(t))
                act.wait_ge(s["q_summed"], freed(t, QV_STEPS))
                act.copy(x_hi, turned).then_inc(s["qv_x_hi"], 1)

            def v_store(i, t, j, r):
                act.wait_ge(s["v_kept"], done(t))
                act.dma_start(dram_rows(values, t, r), stage[0:r, 3 + j, :]).then_inc(v_stored[j], 16)

            def q_rectify(t, r):
                q = tile_of(nodes, t)[0:r, :]
                act.wait_ge(s["q_biased"], done(t))
                act.activation(q, q, ACT.Relu).then_inc(s["q_rect"], 1)

            def q_root(t, j, r):
                act.wait_ge(s["q_stats"], done(t))
                act.activation(stats[0:r, j, 2:3], stats[0:r, j, 2:3], ACT.Sqrt).then_inc(s["q_root"], 1)

            def q_normalise(t, j, r):
                q = tile_of(nodes, t)[0:r, :]
                act.wait_ge(s["q_scaled"], done(t))
                act.activation(q, q, ACT.Relu, scale=stats[0:r, j, 3:4], bias=stats[0:r, j, 4:5],
                               accum_out=column(row_sum, t)[0:r, :]).then_inc(s["q_kept"], 1)

            def qv_round(i, seq, t0, agg_t, steps, r):
                own_chunk(seq, r)
                x_round(t0, 0, r)
                for k in range(PER_TILE + 6):
                    if k < PER_TILE:
                        chunk(seq, k)
                    for j in range(steps):
                        t, at = t0 + j, k - 6 * j
                        if at == 4 and j + 1 < steps:
                            x_round(t + 1, j + 1, r)
                        if at == 5:
                            v_store(i, t, j, r)
                        if at == 7:
                            q_rectify(t, r)
                        if at == 9:
                            q_root(t, j, r)
                        if at == 11:
                            q_normalise(t, j, r)
                extra_chunks(seq, agg_t)
                store_combined(seq, agg_t, r)

            with act.Fori(0, QV_LOOPS) as i:
                qv_round(i, i, i * QV_STEPS, i, QV_STEPS, P)
            qv_round(QV_LOOPS, QV_LOOPS, FULL, FULL, 1, TAIL)

            act.wait_ge(s["angle_ready"], 1)
            act.activation(cos_sin[:, :], cos_sin[:, :], ACT.Sin).then_inc(s["cos_sin_ready"], 1)

            def m_round(sweep, n, slot, v_round, t, r):
                f_hi, v_hi = operands[0:r, 4 * slot, :], operands[0:r, 4 * slot + 2, :]
                act.wait_ge(s["m_summed"], freed(n + sweep * TILES, 2))
                act.copy(f_hi, tile_of(nodes, t)[0:r, :])
                act.wait_ge(mv_loaded[slot], v_round * 16 + 16)
                act.activation(v_hi, stage[0:r, slot, :], ACT.Copy, scale=column(cos_sin, t * 2 + sweep)[0:r, :])\
                    .then_inc(s["m_hi"], 1)

            def moments_hi(sweep):
                for b in range(B):
                    act.wait_ge(s["moment_ready"], 4 * sweep + b + 1)
                    act.copy(weights[:, 2 * sweep, b, :], stage[:, 2 + b, :]).then_inc(s["moment_hi"], 1)

            def m_rounds(sweep, loops, steps, seq0, span):
                with act.Fori(0, loops) as i:
                    seq = i + seq0
                    own_chunk(seq, P)
                    for k in range(PER_TILE):
                        for j in range(steps):
                            if k == j * span:
                                slot = (j + sweep) % 2
                                m_round(sweep, i * steps + (1 + j), slot,
                                        v_rounds(sweep, i, j, steps), i * steps + j, P)
                        chunk(seq, k)
                    extra_chunks(seq, seq - 1)
                    store_combined(seq, seq - 1, P)
                moments_hi(sweep)

            def v_rounds(sweep, i, j, steps):
                if sweep == 0:
                    return i * 2 + (j // 2 + j % 2)
                return i * 3 + (FULL // 2 + 1 + j // 2)

            act.wait_ge(s["cos_sin_ready"], 1)
            act.copy(cs_hi[:, :], cos_sin[:, :]).then_inc(s["cs_rounded"], 1)
            m_round(0, 0, 1, 0, FULL, TAIL)
            m_rounds(0, COS_LOOPS, COS_STEPS, COS_SEQ, 4)
            m_round(1, 0, 0, FULL // 2, FULL, TAIL)
            m_rounds(1, SIN_LOOPS, SIN_STEPS, SIN_SEQ, 3)

            def o_round(n, slot, r):
                turned = banks[1 + slot][:, :].rearrange("p (b c) -> p b c", c=P)[:, :, 0:r]
                f_hi = operands[:, 2 * slot, :].rearrange("p (b c) -> p b c", c=P)[:, :, 0:r]
                act.wait_ge(s["o_turned"], done(n))
                act.wait_ge(s["o_products"], freed(n, 2))
                act.copy(f_hi, turned).then_inc(s["o_hi"], 1)

            def o_first(n, slot, r):
                act.wait_ge(s["o_products"], done(n))
                act.wait_ge(s["o_norm_ready"], done(n))
                act.wait_ge(s["o_stats1"], freed(n, 2))
                act.activation(stage[0:r, 4 + slot, :], banks[3 + 2 * slot][0:r, :], ACT.Copy,
                               scale=stats[0:r, 4 + slot, 4:5]).then_inc(s["o_first"], 1)

            def o_root(n, slot, r, which):
                act.wait_ge(s[f"o_stats{which}"], done(n))
                act.activation(stats[0:r, slot, 2:3], stats[0:r, slot, 2:3], ACT.Sqrt)\
                    .then_inc(s[f"o_root{which}"], 1)

            def o_last(n, slot, t, r):
                act.wait_ge(s["o_final"], done(n))
                act.activation(stage[0:r, 2 + slot, :], stage[0:r, 2 + slot, :], ACT.Identity,
                               scale=stats[0:r, slot, 3:4], bias=stats[0:r, slot, 4:5])\
                    .then_inc(s["o_scaled2"], 1)
                act.wait_ge(s["o_scaled2"], done(n))
                act.dma_start(dram_rows(out, t, r), stage[0:r, 2 + slot, :]).then_inc(o_stored[slot], 16)

            def out_round(n0, t0, seq, agg_t, slots, r):
                steps = len(slots)
                if seq is not None:
                    own_chunk(seq, P)
                o_round(n0, slots[0], r)
                for k in range(4 * steps + 6):
                    if seq is not None and k < PER_TILE:
                        chunk(seq, k)
                    for j, slot in enumerate(slots):
                        n, at = n0 + j, k - 4 * j
                        if at == 2 and j + 1 < steps:
                            o_round(n + 1, slots[j + 1], r)
                        if at == 4:
                            o_first(n, slot, r)
                        if at == 6:
                            o_root(n, slot, r, 1)
                        if at == 8:
                            o_root(n, slot, r, 2)
                        if at == 9:
                            o_last(n, slot, t0 + j, r)
                if seq is not None:
                    for k in range(4 * steps + 6, PER_TILE):
                        chunk(seq, k)
                    extra_chunks(seq, agg_t)
                    store_combined(seq, agg_t, P)

            out_round(0, FULL, OUT_SEQ, OUT_SEQ - 1, [0], TAIL)
            with act.Fori(0, OUT_LOOPS) as i:
                out_round(i * 4 + 1, i * 4, i + (OUT_SEQ + 1), i + OUT_SEQ, [1, 0, 1, 0], P)
            out_round(OUT_LOOPS * 4 + 1, OUT_LOOPS * 4, None, None, [1, 0, 1, 0], P)

        @block.vector
        def _(dve):
            before, here = [0], [0]

            def link(ins, in_stats=False):
                here[0] += 1
                ins.then_inc(s["dve_chain"], 1)
                if in_stats:
                    wait_apart(dve, s["dve_chain"], before[0] + here[0])
                else:
                    dve.wait_ge(s["dve_chain"], before[0] + here[0])

            def chain_round(i, start, per_round):
                before[0], here[0] = i * per_round + start, 0

            def chain_after(start, rounds, per_round):
                assert here[0] == per_round
                before[0], here[0] = start + rounds * per_round, 0

            for name in ("g_x_split", "bins_ready", "chunk_split", "own_split", "gcn_combined", "qv_x_split",
                         "v_kept", "q_biased", "q_stats", "q_scaled", "m_split", "o_split", "o_norm_ready",
                         "o_stats1", "o_stats2", "o_final", "o_mixed", "chunk_hot"):
                dve.sem_inc(s[name], LEAD)
            extras_done = dve.alloc_register("dve_extras")
            dve.reg_mov(extras_done, 0)

            dve.wait_ge(s["consts_set"], 3)
            dve.wait_ge(s["dst_loaded"], 48)
            dve.wait_ge(s["src_loaded"], 48)
            dve.tensor_copy(dst_f, dst_nat).then_inc(s["edges_f"], 1)
            dve.tensor_copy(src_f, src_nat).then_inc(s["edges_f"], 1)
            dve.tensor_copy(ident_r[:, :], ident[:, :]).then_inc(s["ident_ready"], 1)
            dve.memset(plain(zeros_r[:, :]), 0.0).then_inc(s["ident_ready"], 1)
            dve.memset(row_sum[:, :], 0.0)
            dve.memset(ones[:, :], 1.0).then_inc(s["ident_ready"], 1)

            def split_weight(n, hi, lo):
                dve.wait_ge(s["raw_rounded"], n + 1)
                dve.tensor_tensor(lo, raw, plain(hi), ALU.subtract).then_inc(s["raw_split"], 1)

            split_weight(0, g_hi, g_lo)
            for g in range(2 * GROUPS):
                half = slice((g // 2) * P, (g // 2 + 1) * P)
                dve.wait_ge(s["edges_turned"], g + 1)
                dve.tensor_copy((src_cols if g % 2 else dst_cols)[:, half], banks[1 + g % 2][:, 0:P])\
                    .then_inc(s["edges_kept"], 1)
            dve.wait_ge(s["edges_kept"], 2 * GROUPS)
            link(dve.tensor_copy(dst_i, dst_cols[:, :]))
            link(dve.tensor_scalar(mod_i, dst_i, P - 1, None, ALU.bitwise_and))
            link(dve.tensor_scalar(div_i, dst_i, 7, None, ALU.arith_shift_right))
            link(dve.tensor_copy(dst_mod, mod_i))
            link(dve.tensor_copy(dst_div, div_i))
            nat = dst_f.rearrange("p (g e) -> p g e", e=P)
            link(dve.tensor_scalar(neg, dst_f, 0.0, 65536.0, ALU.is_lt, ALU.mult))
            link(dve.tensor_tensor(neg, neg, dst_f, ALU.add))
            link(dve.tensor_reduce(ext[:, 0:GROUPS], neg.rearrange("p (g e) -> p g e", e=P), AX.X, ALU.min))
            link(dve.tensor_reduce(ext[:, GROUPS:], nat, AX.X, ALU.max))
            wide = [P, TILES, GROUPS]
            across = lambda ap: ap.unsqueeze(1).to_broadcast(wide)
            down = lambda ap: ap.unsqueeze(2).to_broadcast(wide)
            link(dve.tensor_tensor(grid, across(ext[:, GROUPS:]), down(first_node[:, :]), ALU.is_ge))
            link(dve.tensor_scalar(small[:, 0:GROUPS], chunk_id, BIG, None, ALU.subtract))
            link(dve.tensor_tensor(grid, grid, across(small[:, 0:GROUPS]), ALU.mult))
            link(dve.tensor_reduce(lim_lo, grid, AX.X, ALU.min))
            link(dve.tensor_scalar(limit, first_node[:, :], float(P), None, ALU.add))
            link(dve.tensor_tensor(grid, across(ext[:, 0:GROUPS]), down(limit), ALU.is_lt))
            link(dve.tensor_scalar(small[:, 0:GROUPS], chunk_id, 1.0, None, ALU.add))
            link(dve.tensor_tensor(grid, grid, across(small[:, 0:GROUPS]), ALU.mult))
            dve.tensor_reduce(lim_hi, grid, AX.X, ALU.max).then_inc(s["limits_ready"], 1)
            dve.wait_ge(s["limits_turned"], 1)
            link(dve.tensor_reduce(col[0:TILES, 0:1], banks[1][0:TILES, 0:P], AX.X, ALU.min))
            link(dve.tensor_reduce(col[0:TILES, 1:2], banks[1][0:TILES, P:2 * P], AX.X, ALU.max))
            link(dve.tensor_scalar(col[0:TILES, 0:1], col[0:TILES, 0:1], BIG, float(CHUNKS - 1), ALU.add, ALU.min))
            link(dve.tensor_scalar(col[0:TILES, 2:3], col[0:TILES, 0:1], float(PER_TILE), None, ALU.add))
            dve.tensor_tensor(col[0:TILES, 1:2], col[0:TILES, 1:2], col[0:TILES, 2:3], ALU.max)\
                .then_inc(s["ranges_ready"], 1)
            dve.wait_ge(s["ranges_turned"], 1)
            dve.tensor_copy(schedule[:, :], banks[2][0:1, 0:2 * TILES]).then_inc(s["schedule_ready"], 1)
            dve.wait_ge(s["schedule_ready"], 1)
            dve.wait_ge(s["bias_loaded"], 48)
            dve.tensor_tensor(bias[:, 1, :], bias[:, 1, :], bias_raw, ALU.add).then_inc(s["setup_done"], 1)
            split_weight(1, weights[:, 0, :, :], weights[:, 1, :, :])
            split_weight(2, weights[:, 2, :, :], weights[:, 3, :, :])

            def bins(t, half):
                c0 = t * HIST + half * HALF[0]
                count = HALF[half]
                cols = lambda ap: (ap[:, c0:c0 + count] if isinstance(t, int) else ap[:, bass.ds(c0, count)])
                dve.wait_ge(s["bins_used"], freed(t * 2 + half, 2))
                dve.tensor_tensor(div_hot[half][:, 0:count, 0:TILES],
                                  iota_bf[:, 0:TILES].unsqueeze(1).to_broadcast([P, count, TILES]),
                                  cols(dst_div).unsqueeze(2).to_broadcast([P, count, TILES]), ALU.is_equal)
                dve.tensor_tensor(mod_hot[half][:, 0:count, :],
                                  iota_bf[:, :].unsqueeze(1).to_broadcast([P, count, P]),
                                  cols(dst_mod).unsqueeze(2).to_broadcast([P, count, P]), ALU.is_equal)\
                    .then_inc(s["bins_ready"], 1)

            def g_split(t, n, r):
                turned = banks[1 + n][:, :].rearrange("p (b c) -> p b c", c=P)[:, :, 0:r]
                x_hi = operands[:, n, :].rearrange("p (b c) -> p b c", c=P)[:, :, 0:r]
                x_lo = operands[:, 2 + n, :].rearrange("p (b c) -> p b c", c=P)[:, :, 0:r]
                dve.wait_ge(s["g_x_hi"], done(t))
                dve.tensor_tensor(x_lo, turned, plain(x_hi), ALU.subtract).then_inc(s["g_x_split"], 1)

            with dve.Fori(0, FULL // 2) as i:
                for n in range(2):
                    g_split(i * 2 + n, n, P)
                    bins(i * 2 + n, 0)
                    bins(i * 2 + n, 1)
            g_split(FULL, 0, TAIL)
            bins(FULL, 0)
            bins(FULL, 1)

            dve.wait_ge(s["degrees_summed"], 1)
            dve.tensor_scalar(dinv[:, :], banks[5][:, 0:TILES], 1.0, 1e-12, ALU.add, ALU.max)\
                .then_inc(s["degrees_kept"], 1)
            dve.wait_ge(s["root_taken"], 1)
            dve.reciprocal(dinv[:, :], dinv[:, :]).then_inc(s["dinv_ready"], 1)
            dve.wait_ge(s["dinv_ready"], 1)
            dve.wait_ge(s["g_kept"], done(FULL))
            with dve.Fori(0, FULL // 4) as i:
                for n in range(4):
                    g = tile_of(nodes, i * 4 + n)
                    dve.tensor_scalar(g, g, column(dinv, i * 4 + n), None, ALU.mult).then_inc(s["g_scaled"], 1)
            g = tile_of(nodes, FULL)[0:TAIL, :]
            dve.tensor_scalar(g, g, dinv[0:TAIL, FULL:FULL + 1], None, ALU.mult).then_inc(s["g_scaled"], 1)

            def tile_nodes(seq, t):
                dve.wait_ge(s["chunk_hot"], freed(chunk_number(seq, 0), 1))
                dve.tensor_scalar(tile_id[:, :], node_id[:, :], column(first_node, t), None, ALU.add)\
                    .then_inc(s["tile_id_ready"], 1)
                dve.wait_ge(s["tile_id_ready"], seq + 1)

            def chunk(seq, k, first):
                n = chunk_number(seq, k)
                dve.wait_ge(s["chunk_summed"], freed(n, SPLIT))
                dve.tensor_scalar(one_hot[:, k % SPLIT, :], tile_id[:, :], column(dst_cols, first + k), None,
                                  ALU.is_equal).then_inc(s["chunk_hot"], 1)
                dve.wait_ge(s["chunk_rounded"], done(n))
                dve.tensor_tensor(lo_ring[k % SPLIT], row_ring[k % RING], plain(hi_ring[k % SPLIT]), ALU.subtract)\
                    .then_inc(s["chunk_split"], 1)

            def own_chunk(seq, r):
                dve.wait_ge(s["own_rounded"], done(seq))
                dve.wait_ge(s["gcn_summed"], freed(seq, 1))
                dve.tensor_tensor(own_lo[0:r, :], own_rows[0:r, :], plain(own_hi)[0:r, :], ALU.subtract)\
                    .then_inc(s["own_split"], 1)

            def begin_tile(seq, t, r):
                first = dve.value_load(column(schedule, t), min_val=0, max_val=CHUNKS - 1)
                tile_nodes(seq, t)
                own_chunk(seq, r)
                return first

            def end_tile(seq, t, r, first):
                end = dve.value_load(column(schedule, t + TILES), min_val=PER_TILE, max_val=CHUNKS - 1 + PER_TILE)
                with dve.If(end > first + PER_TILE):
                    wait_apart(dve, s["chunk_summed"], done(chunk_number(seq, PER_TILE - 1)))
                    with dve.Fori(first + PER_TILE, end) as c:
                        had = dve.snap(extras_done)
                        dve.tensor_scalar(one_hot[:, 0, :], tile_id[:, :], column(dst_cols, c),
                                          None, ALU.is_equal)
                        dve.wait_ge(s["extra_rounded"], had + 1)
                        dve.tensor_tensor(lo_ring[0], row_ring[0], plain(hi_ring[0]), ALU.subtract)\
                            .then_inc(s["extra_split"], 1)
                        dve.wait_ge(s["extra_summed"], had + 1)
                        dve.reg_add(extras_done, extras_done, 1)
                dve.wait_ge(s["combine_loaded"], seq * 16 + 16)
                dve.wait_ge(s["gcn_summed"], done(seq))
                dve.scalar_tensor_tensor(combine[0:r, :], gcn_bank[0:r, :], column(dinv, t)[0:r, :],
                                         combine[0:r, :], ALU.mult, ALU.add).then_inc(s["gcn_combined"], 1)

            def x_split(t, j, r):
                turned = banks[1][:, :].rearrange("p (b c) -> p b c", c=P)[:, :, 0:r]
                x_hi = operands[:, j, :].rearrange("p (b c) -> p b c", c=P)[:, :, 0:r]
                x_lo = operands[:, 3 + j, :].rearrange("p (b c) -> p b c", c=P)[:, :, 0:r]
                dve.wait_ge(s["qv_x_hi"], done(t))
                dve.tensor_tensor(x_lo, turned, plain(x_hi), ALU.subtract).then_inc(s["qv_x_split"], 1)

            def v_keep(i, t, j, r):
                dve.wait_ge(v_stored[j], i * 16)
                dve.wait_ge(s["v_summed"], done(t))
                dve.tensor_tensor(stage[0:r, 3 + j, :], banks[2 + j][0:r, :], bias[0:r, 1, :], ALU.add)\
                    .then_inc(s["v_kept"], 1)

            def q_bias(t, j, r):
                dve.wait_ge(s["q_summed"], done(t))
                dve.tensor_tensor(tile_of(nodes, t)[0:r, :], banks[5 + j][0:r, :], bias[0:r, 0, :], ALU.add)\
                    .then_inc(s["q_biased"], 1)

            def q_variance(t, j, r):
                wait_apart(dve, s["q_rect"], done(t))
                link(dve.bn_stats(bn_parts[0:r, j, :], tile_of(nodes, t)[0:r, :]), True)
                link(dve.bn_aggr(stats[0:r, j, 0:2], bn_parts[0:r, j, :]))
                dve.tensor_scalar(stats[0:r, j, 2:3], stats[0:r, j, 1:2], LN_EPS, None, ALU.add)\
                    .then_inc(s["q_stats"], 1)

            def q_factors(t, j, r):
                dve.wait_ge(s["q_root"], done(t))
                link(dve.reciprocal(stats[0:r, j, 3:4], stats[0:r, j, 2:3]))
                dve.scalar_tensor_tensor(stats[0:r, j, 4:5], stats[0:r, j, 0:1], -1.0, stats[0:r, j, 3:4],
                                         ALU.mult, ALU.mult).then_inc(s["q_scaled"], 1)

            def qv_round(i, seq, t0, agg_t, steps, r):
                first = begin_tile(seq, agg_t, r)
                x_split(t0, 0, r)
                for k in range(PER_TILE + 6):
                    if k < PER_TILE:
                        chunk(seq, k, first)
                    for j in range(steps):
                        t, at = t0 + j, k - 6 * j
                        if at == 2:
                            v_keep(i, t, j, r)
                        if at == 4 and j + 1 < steps:
                            x_split(t + 1, j + 1, r)
                        if at == 5:
                            q_bias(t, j, r)
                        if at == 8:
                            q_variance(t, j, r)
                        if at == 10:
                            q_factors(t, j, r)
                end_tile(seq, agg_t, r, first)

            start = here[0]
            with dve.Fori(0, QV_LOOPS) as i:
                chain_round(i, start, 3 * QV_STEPS)
                qv_round(i, i, i * QV_STEPS, i, QV_STEPS, P)
            chain_after(start, QV_LOOPS, 3 * QV_STEPS)
            qv_round(QV_LOOPS, QV_LOOPS, FULL, FULL, 1, TAIL)

            dve.wait_ge(s["q_kept"], done(FULL))
            h = stage[:, 2, 0:TILES]
            turns = stage[:, 2, 64:64 + TILES]
            link(dve.tensor_tensor(h, row_sum[:, :], row_sum[:, :], ALU.mult))
            for n, op in enumerate((ALU.max, ALU.min)):
                link(dve.tensor_reduce(small[:, n:n + 1], h[:, 0:FULL], AX.X, op))
                link(dve.tensor_tensor(small[0:TAIL, n:n + 1], small[0:TAIL, n:n + 1], h[0:TAIL, FULL:TILES], op))
            dve.tensor_scalar(small[:, 1:2], small[:, 1:2], -1.0, None, ALU.mult).then_inc(s["spread_step"], 1)
            dve.wait_ge(s["extremes_turned"], 1)
            link(dve.tensor_reduce(small[0:1, 2:3], banks[1][0:1, 0:P], AX.X, ALU.max))
            link(dve.tensor_reduce(small[0:1, 3:4], banks[1][0:1, P:2 * P], AX.X, ALU.max))
            link(dve.tensor_tensor(small[0:1, 4:5], small[0:1, 2:3], small[0:1, 3:4], ALU.add))
            link(dve.tensor_scalar(small[0:1, 4:5], small[0:1, 4:5], 4.0, None, ALU.mult))
            link(dve.reciprocal(small[0:1, 5:6], small[0:1, 4:5]))
            dve.tensor_scalar(small[0:1, 6:7], small[0:1, 5:6], PI, None, ALU.mult).then_inc(s["spread_step"], 1)
            dve.wait_ge(s["factor_spread"], 1)
            link(dve.tensor_copy(small[:, 7:8], banks[2][:, 0:1]))
            link(dve.tensor_scalar(h, h, small[:, 7:8], None, ALU.mult))
            link(dve.tensor_scalar(turns, h, 1.0 / (2 * PI), ROUND, ALU.mult, ALU.add))
            link(dve.tensor_scalar(turns, turns, ROUND, None, ALU.subtract))
            for turn in (TURN_HI, TURN_MID, TURN_LO):
                link(dve.scalar_tensor_tensor(h, turns, -turn, h, ALU.mult, ALU.add))
            link(dve.tensor_scalar(h, h, 3.1415925, -3.1415925, ALU.min, ALU.max))
            pair = cos_sin[:, :].rearrange("p (t c) -> p t c", c=2)
            link(dve.tensor_copy(pair[:, :, 1], h))
            link(dve.scalar_tensor_tensor(turns, h, -1.0, h, ALU.mult, ALU.max))
            dve.tensor_scalar(pair[:, :, 0], turns, -1.0, HALF_PI, ALU.mult, ALU.add).then_inc(s["angle_ready"], 1)
            dve.wait_ge(s["cs_rounded"], 1)
            dve.tensor_tensor(cs_lo[:, :], cos_sin[:, :], plain(cs_hi[:, :]), ALU.subtract)\
                .then_inc(s["cs_split"], 1)

            def m_split(sweep, n, slot, t, r):
                f_hi, f_lo = operands[0:r, 4 * slot, :], operands[0:r, 4 * slot + 1, :]
                v_hi, v_lo = operands[0:r, 4 * slot + 2, :], operands[0:r, 4 * slot + 3, :]
                dve.wait_ge(s["m_hi"], done(n + sweep * TILES))
                dve.tensor_tensor(f_lo, tile_of(nodes, t)[0:r, :], plain(f_hi), ALU.subtract)
                dve.scalar_tensor_tensor(v_lo, stage[0:r, slot, :], column(cos_sin, t * 2 + sweep)[0:r, :],
                                         plain(v_hi), ALU.mult, ALU.subtract).then_inc(s["m_split"], 1)

            def moments(sweep):
                dve.wait_ge(s["m_summed"], done(sweep * TILES + FULL))
                dve.wait_ge(s["rows_bias_loaded"], 32)
                if sweep == 0:
                    link(dve.tensor_copy(moment_sums[:, :], banks[7][:, 0:8]))
                    link(dve.tensor_copy(sums_hi[:, :], moment_sums[:, :]))
                    link(dve.tensor_tensor(sums_lo[:, :], moment_sums[:, :], plain(sums_hi[:, :]), ALU.subtract))
                    link(dve.tensor_scalar(moment_sums[:, :], moment_sums[:, :], -1.0, None, ALU.mult))
                else:
                    dve.wait_ge(s["moment_split"], 4)
                for b in range(B):
                    at = 2 * b + sweep
                    dve.scalar_tensor_tensor(stage[:, 2 + b, :], bias[:, 1, :], moment_sums[:, at:at + 1],
                                             banks[3 + b][:, :], ALU.mult, ALU.add).then_inc(s["moment_ready"], 1)
                for b in range(B):
                    dve.wait_ge(s["moment_hi"], 4 * sweep + b + 1)
                    dve.tensor_tensor(weights[:, 2 * sweep + 1, b, :], stage[:, 2 + b, :],
                                      plain(weights[:, 2 * sweep, b, :]), ALU.subtract)\
                        .then_inc(s["moment_split"], 1)

            def m_rounds(sweep, loops, steps, seq0, span):
                with dve.Fori(0, loops) as i:
                    seq = i + seq0
                    first = begin_tile(seq, seq - 1, P)
                    for k in range(PER_TILE):
                        for j in range(steps):
                            if k == j * span:
                                m_split(sweep, i * steps + (1 + j), (j + sweep) % 2, i * steps + j, P)
                        chunk(seq, k, first)
                    end_tile(seq, seq - 1, P, first)
                moments(sweep)

            m_split(0, 0, 1, FULL, TAIL)
            m_rounds(0, COS_LOOPS, COS_STEPS, COS_SEQ, 4)
            m_split(1, 0, 0, FULL, TAIL)
            m_rounds(1, SIN_LOOPS, SIN_STEPS, SIN_SEQ, 3)

            def o_split(n, slot, r):
                turned = banks[1 + slot][:, :].rearrange("p (b c) -> p b c", c=P)[:, :, 0:r]
                f_hi = operands[:, 2 * slot, :].rearrange("p (b c) -> p b c", c=P)[:, :, 0:r]
                f_lo = operands[:, 2 * slot + 1, :].rearrange("p (b c) -> p b c", c=P)[:, :, 0:r]
                dve.wait_ge(s["o_hi"], done(n))
                dve.tensor_tensor(f_lo, turned, plain(f_hi), ALU.subtract).then_inc(s["o_split"], 1)

            def o_norm(n, slot, t, r):
                st = stats[0:r, 4 + slot, :]
                both = banks[7][0:r, 0:2]
                c, sn = column(cos_sin, t * 2)[0:r, :], column(cos_sin, t * 2 + 1)[0:r, :]
                dve.wait_ge(s["o_normed"], done(n))
                link(dve.tensor_scalar(st[:, 0:1], both[:, 0:1], c, None, ALU.mult))
                link(dve.scalar_tensor_tensor(st[:, 1:2], both[:, 1:2], sn, st[:, 0:1], ALU.mult, ALU.add))
                link(dve.tensor_scalar(st[:, 2:3], st[:, 1:2], NORM_EPS, None, ALU.add))
                link(dve.reciprocal(st[:, 3:4], st[:, 2:3]))
                link(dve.tensor_scalar(st[:, 4:5], c, st[:, 3:4], None, ALU.mult))
                dve.tensor_scalar(st[:, 5:6], sn, st[:, 3:4], None, ALU.mult).then_inc(s["o_norm_ready"], 1)

            def mean_variance(slot, r, data):
                link(dve.bn_stats(bn_parts[0:r, slot, :], data), True)
                link(dve.bn_aggr(stats[0:r, slot, 0:2], bn_parts[0:r, slot, :]))
                return dve.tensor_scalar(stats[0:r, slot, 2:3], stats[0:r, slot, 1:2], LN_EPS, None, ALU.add)

            def o_mix(n, slot, loaded, r):
                u, z = stage[0:r, 4 + slot, :], stage[0:r, 2 + slot, :]
                dve.wait_ge(s["o_first"], done(n))
                dve.scalar_tensor_tensor(u, banks[4 + 2 * slot][0:r, :], stats[0:r, 4 + slot, 5:6], u,
                                         ALU.mult, ALU.add).then_inc(s["o_mixed"], 1)
                dve.wait_ge(s["o_mixed"], done(n))
                dve.wait_ge(oc_loaded[slot], loaded)
                link(dve.tensor_tensor(z, z, u, ALU.add), True)
                mean_variance(slot, r, z).then_inc(s["o_stats1"], 1)

            def o_affine(n, slot, loaded, r):
                z, st = stage[0:r, 2 + slot, :], stats[0:r, slot, :]
                dve.wait_ge(s["o_root1"], done(n))
                link(dve.reciprocal(st[:, 3:4], st[:, 2:3]))
                link(dve.scalar_tensor_tensor(z, z, st[:, 0:1], bias[0:r, 0, :], ALU.subtract, ALU.mult))
                link(dve.scalar_tensor_tensor(z, z, st[:, 3:4], bias[0:r, 1, :], ALU.mult, ALU.add))
                dve.wait_ge(ox_loaded[slot], loaded)
                link(dve.scalar_tensor_tensor(z, z, 0.0, stage[0:r, slot, :], ALU.max, ALU.add), True)
                mean_variance(slot, r, z).then_inc(s["o_stats2"], 1)

            def o_factors(n, slot, r):
                st = stats[0:r, slot, :]
                dve.wait_ge(s["o_root2"], done(n))
                link(dve.reciprocal(st[:, 3:4], st[:, 2:3]))
                dve.scalar_tensor_tensor(st[:, 4:5], st[:, 0:1], -1.0, st[:, 3:4], ALU.mult, ALU.mult)\
                    .then_inc(s["o_final"], 1)

            LINKS = 5 + 1 + 2 + 4 + 2 + 1

            def out_round(n0, rounds, t0, seq, agg_t, slots, r):
                steps = len(slots)
                first = begin_tile(seq, agg_t, P) if seq is not None else None
                o_split(n0, slots[0], r)
                for k in range(4 * steps + 6):
                    if seq is not None and k < PER_TILE:
                        chunk(seq, k, first)
                    for j, slot in enumerate(slots):
                        n, at = n0 + j, k - 4 * j
                        loaded = (rounds + (slots[0] + j) // 2) * 16 + 16
                        if at == 2 and j + 1 < steps:
                            o_split(n + 1, slots[j + 1], r)
                        if at == 3:
                            o_norm(n, slot, t0 + j, r)
                        if at == 5:
                            o_mix(n, slot, loaded, r)
                        if at == 7:
                            o_affine(n, slot, loaded, r)
                        if at == 9:
                            o_factors(n, slot, r)
                if seq is not None:
                    for k in range(4 * steps + 6, PER_TILE):
                        chunk(seq, k, first)
                    end_tile(seq, agg_t, P, first)

            dve.wait_ge(s["rows_bias_loaded"], 48)
            out_round(0, 0, FULL, OUT_SEQ, OUT_SEQ - 1, [0], TAIL)
            start = before[0] + here[0]
            with dve.Fori(0, OUT_LOOPS) as i:
                chain_round(i, start, 4 * LINKS)
                out_round(i * 4 + 1, i * 2, i * 4, i + (OUT_SEQ + 1), i + OUT_SEQ, [1, 0, 1, 0], P)
            chain_after(start, OUT_LOOPS, 4 * LINKS)
            out_round(OUT_LOOPS * 4 + 1, OUT_LOOPS * 2, OUT_LOOPS * 4, None, None, [1, 0, 1, 0], P)

        @block.tensor
        def _(pe):
            for name in ("g_x_turned", "g_summed", "bins_used", "chunk_summed", "gcn_summed", "qv_x_turned",
                         "v_summed", "q_summed", "m_summed", "o_turned", "o_normed", "o_products"):
                pe.sem_inc(s[name], LEAD)
            extras_done = pe.alloc_register("pe_extras")
            pe.reg_mov(extras_done, 0)

            def products(out_ap, pairs, start, stop):
                for n, ((a_hi, a_lo), (b_hi, b_lo)) in enumerate(pairs):
                    pe.matmul(out_ap, a_hi, b_hi, start=start and n == 0, stop=False, skip_group_check=True)
                    pe.matmul(out_ap, a_hi, b_lo, start=False, stop=False, skip_group_check=True)
                    last = pe.matmul(out_ap, a_lo, b_hi, start=False, stop=stop and n == len(pairs) - 1,
                                     skip_group_check=True)
                return last

            pe.wait_ge(s["consts_set"], 3)
            pe.wait_ge(s["edges_f"], 2)
            for g in range(2 * GROUPS):
                if g >= 2:
                    pe.wait_ge(s["edges_kept"], g - 1)
                source = src_f if g % 2 else dst_f
                pe.transpose(banks[1 + g % 2][:, 0:P], source[:, (g // 2) * P:(g // 2 + 1) * P], ident[:, :])\
                    .then_inc(s["edges_turned"], 1)
            pe.wait_ge(s["limits_ready"], 1)
            pe.matmul(banks[1][0:TILES, 0:P], lim_lo, ident[:, :], start=True, stop=True)
            pe.matmul(banks[1][0:TILES, P:2 * P], lim_hi, ident[:, :], start=True, stop=True)\
                .then_inc(s["limits_turned"], 1)
            pe.wait_ge(s["ranges_ready"], 1)
            pe.matmul(banks[2][0:1, 0:TILES], col[0:TILES, 0:1], ident[0:TILES, 0:TILES], start=True, stop=True)
            pe.matmul(banks[2][0:1, TILES:2 * TILES], col[0:TILES, 1:2], ident[0:TILES, 0:TILES],
                      start=True, stop=True).then_inc(s["ranges_turned"], 1)
            pe.wait_ge(s["setup_done"], 1)
            pe.wait_ge(s["ident_ready"], 3)

            def turn(bank_, x_in, r):
                for b in range(B):
                    last = pe.transpose(bank_[:, b * P:b * P + r], x_in[0:r, b * P:(b + 1) * P], ident[0:r, 0:r])
                return last

            def g_turn(t, i, n, r):
                pe.wait_ge(g_x_loaded[n], i * 16 + 16)
                pe.wait_ge(s["g_x_split"], freed(t, 2))
                turn(banks[1 + n], stage[:, n, :], r).then_inc(s["g_x_turned"], 1)

            def bins(t, half):
                pe.wait_ge(s["bins_ready"], done(t * 2 + half))
                for c in range(HALF[half]):
                    last = pe.matmul(banks[5][:, 0:TILES], mod_hot[half][:, c, :], div_hot[half][:, c, 0:TILES],
                                     start=False, stop=False, skip_group_check=True)
                last.then_inc(s["bins_used"], 1)

            def g_product(t, n, r):
                pe.wait_ge(s["g_x_split"], done(t))
                pe.wait_ge(s["g_kept"], freed(t, 2))
                pairs = [((operands[:, n, b * P:b * P + r], operands[:, 2 + n, b * P:b * P + r]),
                          (g_hi[:, b, :], g_lo[:, b, :])) for b in range(B)]
                products(banks[3 + n][0:r, :], pairs, True, True).then_inc(s["g_summed"], 1)

            pe.wait_ge(s["raw_split"], 1)
            pe.matmul(banks[5][:, 0:TILES], zero_bf[:, :], zero_bf[:, 0:TILES], start=True, stop=False,
                      skip_group_check=True)
            with pe.Fori(0, FULL // 2) as i:
                g_turn(i * 2, i, 0, P)
                g_turn(i * 2 + 1, i, 1, P)
                for n in range(2):
                    g_product(i * 2 + n, n, P)
                    bins(i * 2 + n, 0)
                    bins(i * 2 + n, 1)
            g_turn(FULL, FULL // 2, 0, TAIL)
            g_product(FULL, 0, TAIL)
            bins(FULL, 0)
            bins(FULL, 1)
            pe.matmul(banks[5][:, 0:TILES], zero_bf[:, :], zero_bf[:, 0:TILES], start=False, stop=True,
                      skip_group_check=True).then_inc(s["degrees_summed"], 1)

            def own_start(seq, r):
                pe.wait_ge(s["own_split"], done(seq))
                pe.wait_ge(s["gcn_combined"], freed(seq, 1))
                pe.matmul(gcn_bank[:, :], ident_r[0:r, :], own_hi[0:r, :], start=True, stop=False,
                          skip_group_check=True)

            def chunk(seq, k):
                slot = k % SPLIT
                pe.wait_ge(s["chunk_split"], done(chunk_number(seq, k)))
                pe.matmul(gcn_bank[:, :], one_hot[:, slot, :], hi_ring[slot], start=False, stop=False,
                          skip_group_check=True)
                pe.matmul(gcn_bank[:, :], one_hot[:, slot, :], lo_ring[slot], start=False, stop=False,
                          skip_group_check=True).then_inc(s["chunk_summed"], 1)

            def own_end(seq, t, r):
                first = pe.value_load(column(schedule, t), min_val=0, max_val=CHUNKS - 1)
                end = pe.value_load(column(schedule, t + TILES), min_val=PER_TILE, max_val=CHUNKS - 1 + PER_TILE)
                with pe.If(end > first + PER_TILE):
                    with pe.Fori(first + PER_TILE, end):
                        had = pe.snap(extras_done)
                        pe.wait_ge(s["extra_split"], had + 1)
                        pe.matmul(gcn_bank[:, :], one_hot[:, 0, :], hi_ring[0], start=False, stop=False,
                                  skip_group_check=True)
                        pe.matmul(gcn_bank[:, :], one_hot[:, 0, :], lo_ring[0], start=False, stop=False,
                                  skip_group_check=True).then_inc(s["extra_summed"], 1)
                        pe.reg_add(extras_done, extras_done, 1)
                pe.matmul(gcn_bank[:, :], ident_r[0:r, :], own_lo[0:r, :], start=False, stop=True,
                          skip_group_check=True).then_inc(s["gcn_summed"], 1)

            def x_turn(t, i, j, r):
                pe.wait_ge(x_loaded[j], i * 16 + 16)
                pe.wait_ge(s["qv_x_split"], freed(t, 1))
                turn(banks[1], stage[:, j, :], r).then_inc(s["qv_x_turned"], 1)

            def x_product(bank_, j, r, blocks, which):
                pairs = [((operands[:, j, b * P:b * P + r], operands[:, 3 + j, b * P:b * P + r]),
                          (weights[:, which, b, :], weights[:, which + 1, b, :])) for b in blocks]
                return products(bank_[0:r, :], pairs, blocks[0] == 0, blocks[-1] == B - 1)

            def qv_round(i, seq, t0, agg_t, steps, r):
                own_r = r
                x_turn(t0, i, 0, r)
                own_start(seq, own_r)
                for k in range(PER_TILE):
                    chunk(seq, k)
                    for j in range(steps):
                        t, at = t0 + j, k - 6 * j
                        if at == 0:
                            pe.wait_ge(s["qv_x_split"], done(t))
                            pe.wait_ge(s["v_kept"], freed(t, QV_STEPS))
                            pe.wait_ge(s["q_biased"], freed(t, QV_STEPS))
                            x_product(banks[2 + j], j, r, [0, 1], 2)
                        if at == 1:
                            x_product(banks[2 + j], j, r, [2, 3], 2).then_inc(s["v_summed"], 1)
                        if at == 2:
                            x_product(banks[5 + j], j, r, [0, 1], 0)
                        if at == 3:
                            if j + 1 < steps:
                                x_turn(t + 1, i, j + 1, r)
                            x_product(banks[5 + j], j, r, [2], 0)
                        if at == 4:
                            x_product(banks[5 + j], j, r, [3], 0).then_inc(s["q_summed"], 1)
                own_end(seq, agg_t, own_r)

            pe.wait_ge(s["raw_split"], 3)
            with pe.Fori(0, QV_LOOPS) as i:
                qv_round(i, i, i * QV_STEPS, i, QV_STEPS, P)
            qv_round(QV_LOOPS, QV_LOOPS, FULL, FULL, 1, TAIL)

            pe.wait_ge(s["spread_step"], 1)
            pe.matmul(banks[1][0:1, 0:P], small[:, 0:1], ident[:, :], start=True, stop=True)
            pe.matmul(banks[1][0:1, P:2 * P], small[:, 1:2], ident[:, :], start=True, stop=True)\
                .then_inc(s["extremes_turned"], 1)
            pe.wait_ge(s["spread_step"], 2)
            pe.matmul(banks[2][:, 0:1], ones[:, :], small[0:1, 6:7], start=True, stop=True)\
                .then_inc(s["factor_spread"], 1)

            def m_products(sweep, slot, t, r, blocks, opening):
                f = operands[0:r, 4 * slot, :], operands[0:r, 4 * slot + 1, :]
                v = operands[0:r, 4 * slot + 2, :], operands[0:r, 4 * slot + 3, :]
                pairs_cs = [ap[0:r, 2 * t:2 * t + 2] if isinstance(t, int) else ap[0:r, bass.ds(t * 2, 2)]
                            for ap in (cs_hi, cs_lo)]
                for b in blocks:
                    f_b = f[0][:, b * P:(b + 1) * P], f[1][:, b * P:(b + 1) * P]
                    last = products(banks[3 + b][:, :], [(f_b, v)], opening, False)
                    if sweep == 0:
                        last = products(banks[7][:, 2 * b:2 * b + 2], [(f_b, pairs_cs)], False, False)
                return last

            def m_rounds(sweep, loops, steps, seq0, span):
                with pe.Fori(0, loops) as i:
                    seq = i + seq0
                    own_start(seq, P)
                    for k in range(PER_TILE):
                        chunk(seq, k)
                        for j in range(steps):
                            at = k - span * j
                            if at == 0:
                                pe.wait_ge(s["m_split"], done(i * steps + (1 + j + sweep * TILES)))
                            if 0 <= at < span:
                                blocks = [at] if span == 4 else ([0, 1], [2], [3])[at]
                                last = m_products(sweep, (j + sweep) % 2, i * steps + j, P, blocks, False)
                                if at == span - 1:
                                    last.then_inc(s["m_summed"], 1)
                    own_end(seq, seq - 1, P)

            pe.wait_ge(s["v_kept"], done(FULL))
            pe.wait_ge(s["q_biased"], done(FULL))
            pe.wait_ge(s["cs_split"], 1)
            pe.matmul(banks[7][:, 0:8], ident_r[:, :], zeros_r[:, :], start=True, stop=False, skip_group_check=True)
            pe.wait_ge(s["m_split"], done(0))
            m_products(0, 1, FULL, TAIL, range(B), True).then_inc(s["m_summed"], 1)
            m_rounds(0, COS_LOOPS, COS_STEPS, COS_SEQ, 4)
            pe.wait_ge(s["moment_ready"], 4)
            pe.wait_ge(s["m_split"], done(TILES))
            m_products(1, 0, FULL, TAIL, range(B), True).then_inc(s["m_summed"], 1)
            m_rounds(1, SIN_LOOPS, SIN_STEPS, SIN_SEQ, 3)

            def o_turn(n, fours, place, slot, r):
                pe.wait_ge(oq_loaded[place % 4], (fours + place // 4) * 16 + 16)
                pe.wait_ge(s["o_split"], freed(n, 2))
                turn(banks[1 + slot], plain(operands[:, 4 + place % 4, :]), r).then_inc(s["o_turned"], 1)

            def o_pairs(slot, r, blocks):
                hi, lo = operands[:, 2 * slot, :], operands[:, 2 * slot + 1, :]
                return [(hi[:, b * P:b * P + r], lo[:, b * P:b * P + r]) for b in blocks]

            def o_norms(n, slot, r):
                pe.wait_ge(s["o_norm_ready"], freed(n, 1))
                pairs = [(f, (sums_hi[:, 2 * b:2 * b + 2], sums_lo[:, 2 * b:2 * b + 2]))
                         for b, f in enumerate(o_pairs(slot, r, range(B)))]
                products(banks[7][0:r, 0:2], pairs, True, True).then_inc(s["o_normed"], 1)

            def o_product(which, slot, r, blocks):
                pairs = [(f, (weights[:, 2 * which, b, :], weights[:, 2 * which + 1, b, :]))
                         for b, f in zip(blocks, o_pairs(slot, r, blocks))]
                return products(banks[3 + 2 * slot + which][0:r, :], pairs, blocks[0] == 0, blocks[-1] == B - 1)

            def out_round(n0, fours, seq, agg_t, slots, r):
                steps = len(slots)
                o_turn(n0, fours, slots[0], slots[0], r)
                if seq is not None:
                    own_start(seq, P)
                for k in range(max(4 * steps, PER_TILE if seq is not None else 0)):
                    if seq is not None:
                        if k < PER_TILE:
                            chunk(seq, k)
                    for j, slot in enumerate(slots):
                        n, at = n0 + j, k - 4 * j
                        if at == 0:
                            pe.wait_ge(s["o_split"], done(n))
                            pe.wait_ge(s["o_mixed"], freed(n, 2))
                            o_norms(n, slot, r)
                            o_product(0, slot, r, [0, 1])
                        if at == 1:
                            if j + 1 < steps:
                                o_turn(n + 1, fours, slots[0] + j + 1, slots[j + 1], r)
                            o_product(0, slot, r, [2, 3])
                        if at == 2:
                            o_product(1, slot, r, [0, 1])
                        if at == 3:
                            o_product(1, slot, r, [2, 3]).then_inc(s["o_products"], 1)
                if seq is not None:
                    own_end(seq, agg_t, P)

            pe.wait_ge(s["moment_split"], 8)
            out_round(0, 0, OUT_SEQ, OUT_SEQ - 1, [0], TAIL)
            with pe.Fori(0, OUT_LOOPS) as i:
                out_round(i * 4 + 1, i, i + (OUT_SEQ + 1), i + OUT_SEQ, [1, 0, 1, 0], P)
            out_round(OUT_LOOPS * 4 + 1, OUT_LOOPS, None, None, [1, 0, 1, 0], P)


_INS = ["x", "src", "dst", "L0_gnn_Wq", "L0_gnn_bq", "L0_gnn_Wv", "L0_gnn_bv", "L0_gnn_Wg", "L0_gnn_bg",
        "L0_gnn_gamma", "L0_gnn_beta"]


def kernel(**inputs):
    import concourse.bacc as bacc
    from concourse.bass_utils import run_bass_kernel_spmd

    nc = bacc.Bacc("TRN2", target_bir_lowering=False, num_devices=1)
    arrays, args = {}, []
    for name in _INS:
        a = np.ascontiguousarray(inputs[name])
        arrays[f"in_{name}"] = a
        args.append(nc.dram_tensor(f"in_{name}", a.shape, mybir.dt.from_np(a.dtype), kind="ExternalInput").ap())
    out = nc.dram_tensor("out", inputs["x"].shape, F32, kind="ExternalOutput").ap()
    build_layer(nc, *args, out)
    r = run_bass_kernel_spmd(nc, [arrays], core_ids=[0])
    return r.results[0]["out"]
```

```python
from contextlib import ExitStack

import numpy as np
import concourse.bass as bass
from concourse import mybir

F32 = mybir.dt.float32
F32R = mybir.dt.float32r
BF16 = mybir.dt.bfloat16
I32 = mybir.dt.int32
U32 = mybir.dt.uint32
U16 = mybir.dt.uint16
ALU = mybir.AluOpType
ACT = mybir.ActivationFunctionType
AX = mybir.AxisListType

P = 128
LEAD = 18
BIG = 4096.0
PI = float(np.pi)
TURN_HI = 6.28125
TURN_MID = float(np.float32(2 * np.pi - 6.28125))
TURN_LO = float(2 * np.pi - 6.28125 - TURN_MID)
ROUND = 12582912.0
HALF_PI = float(np.float32(np.pi / 2))


def done(n):
    return n + (1 + LEAD)


def freed(n, depth):
    return n + (1 + LEAD - depth)


def build_layer(nc, x, src, dst, Wq, bq, Wv, bv, Wg, bg, gamma, beta, out):
    N, D = x.shape
    E = src.shape[0]
    B = D // P
    TILES = -(-N // P)
    FULL = N // P
    TAIL = N - FULL * P
    CHUNKS = -(-E // P)
    GROUPS = -(-CHUNKS // P)
    HIST = -(-CHUNKS // TILES)
    PER_TILE = 18
    RING = 9
    SPLIT = 3
    BATCH = 6
    COLS = GROUPS * P
    LN_EPS = 1e-5
    NORM_EPS = 1e-10
    QV_STEPS, COS_STEPS, SIN_STEPS, OUT_STEPS = 3, 4, 6, 4
    QV_LOOPS, COS_LOOPS, SIN_LOOPS = FULL // 3, FULL // 4, FULL // 6
    OUT_LOOPS = FULL // 4
    COS_SEQ = QV_LOOPS + 1
    SIN_SEQ = COS_SEQ + COS_LOOPS
    OUT_SEQ = SIN_SEQ + SIN_LOOPS
    assert B == 4 and TAIL and FULL == 48 and OUT_SEQ + OUT_LOOPS == TILES
    assert HIST * TILES <= COLS and CHUNKS + PER_TILE <= COLS and PER_TILE % RING == 0 == PER_TILE % BATCH

    table = nc.dram_tensor("scaled_g", [TILES * P, D], F32).ap()
    values = nc.dram_tensor("values", [TILES * P, D], F32).ap()
    combined = nc.dram_tensor("gcn_plus_values", [TILES * P, D], F32).ap()

    ctx = ExitStack()
    with ctx:
        def sb(name, shape, dt):
            return ctx.enter_context(nc.sbuf_tensor(name, shape, dt))

        def sem(name):
            return ctx.enter_context(nc.semaphore(name))

        def bank(name):
            return ctx.enter_context(nc.psum_tensor(name, [P, D], F32))

        nodes = sb("nodes", [P, TILES * D], F32)
        weights = sb("weights", [P, 4, B, D], F32R)
        split = sb("split", [P, 8, D], F32R)
        rows = sb("rows", [P, 4, D], F32R)
        operands = sb("operands", [P, 8, D], F32R)
        stage = sb("stage", [P, 6, D], F32)
        own_rows = sb("own_rows", [P, D], F32)
        combine = sb("combine", [P, D], F32)
        mix = sb("mix", [P, D], F32)
        bias = sb("bias", [P, 2, D], F32)
        src_cols = sb("src_cols", [P, COLS], U16)
        dst_cols = sb("dst_cols", [P, COLS], F32)
        index_slots = sb("index_slots", [P, PER_TILE], U32)
        one_hot = sb("one_hot", [P, SPLIT, P], F32R)
        ident = sb("ident", [P, P], F32)
        ident_r = sb("ident_r", [P, P], F32R)
        node_id = sb("node_id", [P, P], F32)
        tile_id = sb("tile_id", [P, P], F32)
        zeros_r = sb("zeros_r", [P, P], F32R)
        dinv = sb("dinv", [P, TILES], F32)
        cos_sin = sb("cos_sin", [P, 2 * TILES], F32)
        row_sum = sb("row_sum", [P, TILES], F32)
        schedule = sb("schedule", [1, 2 * TILES], I32)
        stats = sb("stats", [P, 6, 8], F32)
        moment_sums = sb("moment_sums", [P, 8], F32)
        sums_hi = sb("sums_hi", [P, 8], F32R)
        sums_lo = sb("sums_lo", [P, 8], F32R)
        cs_hi = sb("cs_hi", [P, 2 * TILES], F32R)
        cs_lo = sb("cs_lo", [P, 2 * TILES], F32R)
        bn_parts = sb("bn_parts", [P, 3, 6], F32)
        small = sb("small", [P, 16], F32)
        first_node = sb("first_node", [P, TILES], F32)
        ones = sb("ones", [1, P], F32)

        banks = [bank(f"bank{n}") for n in range(8)]
        gcn_bank = banks[0]

        scratch = nodes[:, 0:16 * COLS]
        part = lambda n, w=COLS: nodes[:, n * COLS:n * COLS + w]
        dst_nat = part(0).bitcast(I32)
        src_nat = part(1).bitcast(I32)
        dst_f = part(2)
        src_f = part(3)
        dst_i = part(4).bitcast(I32)
        mod_i = part(5).bitcast(I32)
        div_i = part(6).bitcast(I32)
        neg = part(7)
        bias_raw = part(8, D)
        bins = stage[:, 2, :]
        chunk_id = nodes[:, 9 * COLS:9 * COLS + GROUPS]
        limit = nodes[:, 10 * COLS:10 * COLS + TILES]
        grid = nodes[:, 11 * COLS:11 * COLS + TILES * GROUPS].rearrange("p (t g) -> p t g", g=GROUPS)
        ext = nodes[:, 12 * COLS:12 * COLS + 2 * GROUPS]
        lim_lo = nodes[:, 13 * COLS:13 * COLS + TILES]
        lim_hi = nodes[:, 13 * COLS + 64:13 * COLS + 64 + TILES]
        col = nodes[:, 14 * COLS:14 * COLS + 8]
        dst_mod = combine[:, :].bitcast(BF16)[:, 0:COLS]
        dst_div = own_rows[:, :].bitcast(BF16)[:, 0:COLS]
        HALF = (-(-HIST // 2), HIST // 2)
        mod_hot = [stage[:, 2:6, :].rearrange("p a d -> p (a d)")[:, h * HALF[0] * 64:(h + 1) * HALF[0] * 64]
                   .bitcast(BF16).rearrange("p (c j) -> p c j", j=P) for h in range(2)]
        DIVW = TILES + 1
        div_base = 2 * HALF[0] * 64
        div_hot = [stage[:, 2:6, :].rearrange("p a d -> p (a d)")
                   [:, div_base + h * HALF[0] * DIVW // 2:div_base + (h + 1) * HALF[0] * DIVW // 2]
                   .bitcast(BF16).rearrange("p (c j) -> p c j", j=DIVW) for h in range(2)]
        iota_bf = sb("iota_bf", [P, P], BF16)
        zero_bf = sb("zero_bf", [P, P], BF16)

        raws = [nodes[:, (32 + n * B) * D:(32 + (n + 1) * B) * D].rearrange("p (k n) -> p k n", n=D)
                for n in range(3)]
        g_hi, g_lo = split[:, 0:4, :], split[:, 4:8, :]
        hi_ring = [split[:, n, :] for n in range(SPLIT)]
        row_ring = [split[:, SPLIT + n, :] if n < 5 else rows[:, n - 5, :] for n in range(RING)]

        def plain(ap):
            return ap.bitcast(F32)

        def tile_of(ap, t, w=D):
            return ap[:, t * w:(t + 1) * w] if isinstance(t, int) else ap[:, bass.ds(t * w, w)]

        def dram_rows(ap, t, r):
            return ap[t * P:t * P + r, :] if isinstance(t, int) else ap[bass.ds(t * P, r), :]

        def column(ap, c):
            return ap[:, c:c + 1] if isinstance(c, int) else ap[:, bass.ds(c, 1)]

        s = {}
        for name in (
            "setup_done", "pads_set", "dst_loaded", "src_loaded", "bias_loaded", "g_x_turned",
            "g_scaled", "table_written", "own_added", "own_loaded", "combined_stored",
            "combine_loaded", "qv_x_turned", "m_split", "v_kept", "q_biased", "rows_bias_loaded",
            "moment_split", "o_turned", "consts_set", "chunk_indexed", "extra_indexed",
            "chunk_rounded", "chunk_summed", "extra_landed", "extra_summed", "raw_rounded",
            "g_summed", "g_x_hi", "g_kept", "degrees_kept", "root_taken", "extra_rounded",
            "gcn_combined", "q_summed", "qv_x_hi", "q_rect", "q_stats", "q_root", "q_scaled",
            "q_kept", "angle_ready", "cos_sin_ready", "m_summed", "m_hi", "moment_ready",
            "moment_hi", "cs_rounded", "o_products", "o_hi", "o_norm_ready", "o_stats1", "o_first",
            "o_final", "o_scaled2", "dve_chain", "edges_f", "ident_ready", "raw_split",
            "edges_turned", "edges_kept", "limits_ready", "limits_turned", "ranges_ready",
            "ranges_turned", "schedule_ready", "bins_used", "bins_ready", "g_x_split",
            "degrees_summed", "dinv_ready", "chunk_hot", "tile_id_ready", "chunk_split",
            "extra_split", "gcn_summed", "qv_x_split", "v_summed", "spread_step", "extremes_turned",
            "factor_spread", "cs_split", "o_split", "o_normed", "o_mixed", "o_root1", "o_stats2",
            "o_root2", "variance_linked", "factors_linked", "norm_linked", "mix_linked",
            "affine_linked", "o_factors_linked", "g_raw_loaded", "q_raw_loaded", "v_raw_loaded",
        ):
            s[name] = sem(name)
        landed = [sem(f"row_landed{n}") for n in range(RING)]
        g_x_loaded = [sem(f"g_x_loaded{n}") for n in range(2)]
        x_loaded = [sem(f"x_loaded{n}") for n in range(3)]
        v_stored = [sem(f"v_stored{n}") for n in range(3)]
        mv_loaded = [sem(f"mv_loaded{n}") for n in range(2)]
        ox_loaded = [sem(f"ox_loaded{n}") for n in range(2)]
        oc_loaded = [sem(f"oc_loaded{n}") for n in range(4)]
        oq_loaded = [sem(f"oq_loaded{n}") for n in range(2)]
        o_stored = [sem(f"o_stored{n}") for n in range(4)]

        block = ctx.enter_context(nc.Block())

        def wait_apart(eng, semaphore, value):
            value = eng.to_reg(value) if not isinstance(value, int) else value
            eng.wait_ge(s["setup_done"], 1)
            eng.wait_ge(semaphore, value)

        def chunk_number(seq, k):
            return seq * PER_TILE + k

        def exists(n):
            return not isinstance(n, int) or n >= 0

        def after_last(n):
            return isinstance(n, int) and n > FULL

        def in_flight(k, i, steps, span):
            for back in (1, 0):
                for j in range(steps):
                    at = k - span * j + PER_TILE * back
                    if exists(i - back) and at >= 0 and not after_last((i - back) * steps + j):
                        yield (i - back) * steps + j, j, at

        @block.sync
        def _(sp):
            sp.wait_ge(s["pads_set"], 1)
            for ap, nat, arrived in ((dst, dst_nat, s["dst_loaded"]), (src, src_nat, s["src_loaded"])):
                view = nat.rearrange("p (g e) -> p g e", e=P)
                whole = (GROUPS - 1) * P
                left = E // P - whole
                sp.dma_start(view[:, 0:GROUPS - 1, :],
                             ap[0:whole * P].rearrange("(g p e) -> p g e", p=P, e=P)).then_inc(arrived, 16)
                sp.dma_start(view[0:left, GROUPS - 1, :],
                             ap[whole * P:(whole + left) * P].rearrange("(p e) -> p e", e=P)).then_inc(arrived, 16)
                sp.dma_start(view[left:left + 1, GROUPS - 1, 0:E - E // P * P],
                             ap[E // P * P:E].rearrange("(p e) -> p e", p=1)).then_inc(arrived, 16)
            for raw, weight, arrived in zip(raws, (Wg, Wq, Wv), ("g_raw_loaded", "q_raw_loaded", "v_raw_loaded")):
                sp.dma_start(raw, weight.rearrange("(k p) n -> p k n", p=P)).then_inc(s[arrived], 16)
            row = lambda v: v.rearrange("(a n) -> a n", a=1).to_broadcast([P, D])
            sp.dma_start(bias[:, 0, :], row(bq)).then_inc(s["bias_loaded"], 16)
            sp.dma_start(bias[:, 1, :], row(bv)).then_inc(s["bias_loaded"], 16)
            sp.dma_start(bias_raw, row(bg)).then_inc(s["bias_loaded"], 16)
            def g_load(n, t, r):
                sp.wait_ge(s["g_x_turned"], freed(t, 2))
                sp.dma_start(stage[0:r, n, :], dram_rows(x, t, r)).then_inc(g_x_loaded[n], 16)

            with sp.Fori(0, FULL // 2) as i:
                g_load(0, i * 2, P)
                g_load(1, i * 2 + 1, P)
            g_load(0, FULL, TAIL)

            with sp.Fori(0, TILES) as t:
                sp.wait_ge(s["g_scaled"], t + 1)
                sp.dma_start(dram_rows(table, t, P), tile_of(nodes, t)).then_inc(s["table_written"], 16)
            sp.wait_ge(s["table_written"], 16 * TILES)

            def own_load(seq):
                sp.wait_ge(s["own_added"], freed(seq, 1))
                sp.dma_start(own_rows[:, :], dram_rows(table, seq, P)).then_inc(s["own_loaded"], 16)

            def combine_load(seq):
                sp.wait_ge(s["combined_stored"], seq * 16)
                sp.dma_start(combine[:, :], dram_rows(values, seq, P)).then_inc(s["combine_loaded"], 16)

            def x_load(t, j, r):
                sp.wait_ge(s["qv_x_turned"], freed(t, QV_STEPS))
                sp.dma_start(stage[0:r, j, :], dram_rows(x, t, r)).then_inc(x_loaded[j], 16)

            def v_is_stored(i):
                sp.wait_ge(v_stored[0], i * 16 + 16)
                sp.wait_ge(v_stored[1], i * 16)
                sp.wait_ge(v_stored[2], i * 16)

            for j in range(QV_STEPS):
                x_load(j, j, P)
            with sp.Fori(0, QV_LOOPS - 1) as i:
                own_load(i)
                x_load((i + 1) * QV_STEPS, 0, P)
                v_is_stored(i)
                combine_load(i)
                x_load((i + 1) * QV_STEPS + 1, 1, P)
                x_load((i + 1) * QV_STEPS + 2, 2, P)
            own_load(QV_LOOPS - 1)
            x_load(FULL, 0, TAIL)
            v_is_stored(QV_LOOPS - 1)
            combine_load(QV_LOOPS - 1)
            own_load(QV_LOOPS)
            v_is_stored(QV_LOOPS)
            combine_load(QV_LOOPS)

            def v_load(g, slot, t):
                sp.wait_ge(s["m_split"], freed(g, 2))
                sp.dma_start(stage[:, slot, :], dram_rows(values, t, P)).then_inc(mv_loaded[slot], 16)

            def v_loads(sweep, loops, steps, seq0):
                with sp.Fori(0, loops) as i:
                    own_load(i + seq0)
                    for j in range(steps):
                        if j == steps - 1:
                            combine_load(i + seq0)
                        v_load(i * steps + (1 + j + sweep * TILES), (1 + j + sweep) % 2, i * steps + (1 + j))

            sp.wait_ge(s["v_kept"], done(TILES - 1))
            sp.wait_ge(s["q_biased"], done(TILES - 1))
            sp.dma_start(bias[:, 1, :], row(bg)).then_inc(s["rows_bias_loaded"], 16)
            sp.dma_start(bias[:, 0, :], row(gamma)).then_inc(s["rows_bias_loaded"], 16)
            v_load(0, 0, 0)
            v_loads(0, COS_LOOPS, COS_STEPS, COS_SEQ)
            v_load(TILES, 1, 0)
            v_loads(1, SIN_LOOPS, SIN_STEPS, SIN_SEQ)

            sp.wait_ge(s["moment_split"], 8)
            sp.dma_start(bias[:, 1, :], row(beta)).then_inc(s["rows_bias_loaded"], 16)

            def f_load(n):
                slot = n % 2
                sp.wait_ge(s["o_turned"], freed(n, 2))
                sp.dma_start(plain(operands[:, 4 + slot, :]), tile_of(nodes, n)).then_inc(oq_loaded[slot], 16)

            def out_loads(i, j, r):
                n = i * OUT_STEPS + j
                sp.wait_ge(o_stored[j], i * 16)
                sp.wait_ge(s["combined_stored"], n * 16 + 16)
                sp.dma_start(stage[:, 2 + j, :], dram_rows(combined, n, P)).then_inc(oc_loaded[j], 16)
                sp.wait_ge(s["o_stats2"], freed(n, 2))
                sp.dma_start(stage[0:r, j % 2, :], dram_rows(x, n, r)).then_inc(ox_loaded[j % 2], 16)

            def out_round(i, last):
                own_load(i + OUT_SEQ)
                for j in range(OUT_STEPS):
                    if not last or j < 3:
                        n, slot = i * OUT_STEPS + (j + 2), j % 2
                        sp.wait_ge(s["o_turned"], freed(n, 2))
                        sp.dma_start(plain(operands[:, 4 + slot, :]), tile_of(nodes, n))\
                            .then_inc(oq_loaded[slot], 16)
                    if j == 2:
                        combine_load(i + OUT_SEQ)
                    out_loads(i, j, P)

            f_load(0)
            f_load(1)
            with sp.Fori(0, OUT_LOOPS - 1) as i:
                out_round(i, False)
            out_round(OUT_LOOPS - 1, True)
            out_loads(OUT_LOOPS, 0, TAIL)
            sp.wait_ge(o_stored[0], 16 * (OUT_LOOPS + 1))
            for j in range(1, OUT_STEPS):
                sp.wait_ge(o_stored[j], 16 * OUT_LOOPS)

        @block.gpsimd
        def _(pool):
            pool.memset(dst_nat, -1)
            pool.memset(src_nat, 0).then_inc(s["pads_set"], 1)
            pool.memset(ident[:, :], 0.0).then_inc(s["consts_set"], 1)
            pool.wait_ge(s["consts_set"], 1)
            pool.affine_select(out=ident[:, :], in_=ident[:, :], compare_op=ALU.not_equal, fill=1.0, base=0,
                               pattern=[[-1, P]], channel_multiplier=1).then_inc(s["consts_set"], 1)
            pool.iota(node_id[:, :], pattern=[[1, P]], base=0, channel_multiplier=0,
                      allow_small_or_imprecise_dtypes=True)
            pool.iota(iota_bf[:, :], pattern=[[1, P]], base=0, channel_multiplier=0,
                      allow_small_or_imprecise_dtypes=True)
            pool.iota(chunk_id, pattern=[[P, GROUPS]], base=0, channel_multiplier=1,
                      allow_small_or_imprecise_dtypes=True)
            pool.iota(first_node[:, :], pattern=[[P, TILES]], base=0, channel_multiplier=0,
                      allow_small_or_imprecise_dtypes=True)
            pool.memset(zero_bf[:, :], 0.0).then_inc(s["consts_set"], 1)
            pool.sem_inc(s["chunk_indexed"], LEAD)
            pool.sem_inc(s["extra_indexed"], LEAD)

            pool.wait_ge(s["setup_done"], 1)
            pool.wait_ge(s["table_written"], 16 * TILES)
            extras_done = pool.alloc_register("pool_extras")
            pool.reg_mov(extras_done, 0)

            def gather_tile(seq):
                first = pool.value_load(column(schedule, seq), min_val=0, max_val=CHUNKS - 1)
                for k in range(PER_TILE):
                    if k % BATCH == 0:
                        wait_apart(pool, s["chunk_rounded"], freed(chunk_number(seq, k + BATCH - 1), PER_TILE))
                        pool.tensor_copy(index_slots[:, k:k + BATCH], src_cols[:, bass.ds(first + k, BATCH)])\
                            .then_inc(s["chunk_indexed"], 1)
                        pool.wait_ge(s["chunk_indexed"], done(seq * (PER_TILE // BATCH) + k // BATCH))
                    wait_apart(pool, s["chunk_summed"], freed(chunk_number(seq, k), RING))
                    pool.indirect_dma_start(
                        out=plain(row_ring[k % RING]), out_offset=None, in_=table,
                        in_offset=bass.IndirectOffsetOnAxis(ap=index_slots[:, k:k + 1], axis=0)
                    ).then_inc(landed[k % RING], 16)
                end = pool.value_load(column(schedule, seq + TILES), min_val=PER_TILE, max_val=CHUNKS - 1 + PER_TILE)
                with pool.If(end > first + PER_TILE):
                    wait_apart(pool, s["chunk_summed"], done(chunk_number(seq, PER_TILE - 1)))
                    with pool.Fori(first + PER_TILE, end) as c:
                        had = pool.snap(extras_done)
                        pool.tensor_copy(index_slots[:, 0:1], column(src_cols, c))\
                            .then_inc(s["extra_indexed"], 1)
                        wait_apart(pool, s["extra_indexed"], had + (1 + LEAD))
                        pool.indirect_dma_start(
                            out=plain(row_ring[0]), out_offset=None, in_=table,
                            in_offset=bass.IndirectOffsetOnAxis(ap=index_slots[:, 0:1], axis=0)
                        ).then_inc(s["extra_landed"], 16)
                        pool.wait_ge(s["extra_summed"], had + 1)
                        pool.reg_add(extras_done, extras_done, 1)

            with pool.Fori(0, TILES) as seq:
                gather_tile(seq)

        @block.scalar
        def _(act):
            for name in ("g_x_hi", "g_kept", "chunk_rounded", "qv_x_hi", "q_rect", "q_root",
                         "q_kept", "m_hi", "o_hi", "o_first", "o_root1", "o_root2", "o_scaled2"):
                act.sem_inc(s[name], LEAD)
            extras_done = act.alloc_register("act_extras")
            act.reg_mov(extras_done, 0)

            for n, (name, hi) in enumerate((("g_raw_loaded", g_hi), ("q_raw_loaded", weights[:, 0, :, :]),
                                            ("v_raw_loaded", weights[:, 2, :, :]))):
                act.wait_ge(s[name], 16)
                act.copy(hi, raws[n]).then_inc(s["raw_rounded"], 1)

            def g_step(t, n, r):
                turned = banks[1 + n][:, :].rearrange("p (b c) -> p b c", c=P)[:, :, 0:r]
                x_hi = operands[:, n, :].rearrange("p (b c) -> p b c", c=P)[:, :, 0:r]
                act.wait_ge(s["g_x_turned"], done(t))
                act.wait_ge(s["g_summed"], freed(t, 2))
                act.copy(x_hi, turned).then_inc(s["g_x_hi"], 1)

            def g_keep(t, n, r):
                act.wait_ge(s["g_summed"], done(t))
                act.copy(tile_of(nodes, t)[0:r, :], banks[3 + n][0:r, :]).then_inc(s["g_kept"], 1)

            act.wait_ge(s["setup_done"], 1)
            with act.Fori(0, FULL // 2) as i:
                g_step(i * 2, 0, P)
                g_step(i * 2 + 1, 1, P)
                g_keep(i * 2, 0, P)
                g_keep(i * 2 + 1, 1, P)
            g_step(FULL, 0, P)
            g_keep(FULL, 0, P)
            act.wait_ge(s["degrees_kept"], 1)
            act.activation(dinv[:, :], dinv[:, :], ACT.Sqrt).then_inc(s["root_taken"], 1)

            def chunk(seq, k):
                n = chunk_number(seq, k)
                act.wait_ge(landed[k % RING], seq * (16 * PER_TILE // RING) + 16 * (k // RING + 1))
                act.wait_ge(s["chunk_summed"], freed(n, SPLIT))
                act.copy(hi_ring[k % SPLIT], plain(row_ring[k % RING])).then_inc(s["chunk_rounded"], 1)

            def extra_chunks(seq):
                first = act.value_load(column(schedule, seq), min_val=0, max_val=CHUNKS - 1)
                end = act.value_load(column(schedule, seq + TILES), min_val=PER_TILE, max_val=CHUNKS - 1 + PER_TILE)
                with act.If(end > first + PER_TILE):
                    wait_apart(act, s["chunk_summed"], done(chunk_number(seq, PER_TILE - 1)))
                    with act.Fori(first + PER_TILE, end):
                        had = act.snap(extras_done)
                        act.wait_ge(s["extra_landed"], had * 16 + 16)
                        act.copy(hi_ring[0], plain(row_ring[0])).then_inc(s["extra_rounded"], 1)
                        act.wait_ge(s["extra_summed"], had + 1)
                        act.reg_add(extras_done, extras_done, 1)

            def store_combined(seq):
                if exists(seq):
                    act.wait_ge(s["gcn_combined"], done(seq))
                    act.dma_start(dram_rows(combined, seq, P), combine[:, :]).then_inc(s["combined_stored"], 16)

            def x_round(t, j):
                act.wait_ge(s["qv_x_turned"], done(t))
                act.wait_ge(s["q_summed"], freed(t, QV_STEPS))
                act.copy(operands[:, j, :], banks[1][:, :]).then_inc(s["qv_x_hi"], 1)

            def v_store(t, j):
                act.wait_ge(s["v_kept"], done(t))
                act.dma_start(dram_rows(values, t, P), stage[:, 3 + j, :]).then_inc(v_stored[j], 16)

            def q_rectify(t):
                q = tile_of(nodes, t)
                act.wait_ge(s["q_biased"], done(t))
                act.activation(q, q, ACT.Relu).then_inc(s["q_rect"], 1)

            def q_root(t, j):
                act.wait_ge(s["q_stats"], done(t))
                act.activation(stats[:, j, 2:3], stats[:, j, 2:3], ACT.Sqrt).then_inc(s["q_root"], 1)

            def q_normalise(t, j):
                q = tile_of(nodes, t)
                act.wait_ge(s["q_scaled"], done(t))
                act.activation(q, q, ACT.Relu, scale=stats[:, j, 3:4], bias=stats[:, j, 4:5],
                               accum_out=column(row_sum, t)).then_inc(s["q_kept"], 1)

            def qv_round(i):
                for k in range(PER_TILE):
                    chunk(i, k)
                    if k == 3:
                        store_combined(i - 1)
                    for t, j, at in in_flight(k, i, QV_STEPS, 6):
                        if at == 5 and not after_last(t + 1):
                            x_round(t + 1, (j + 1) % QV_STEPS)
                        if at == 6:
                            v_store(t, j)
                        if at == 9:
                            q_rectify(t)
                        if at == 12:
                            q_root(t, j)
                        if at == 15:
                            q_normalise(t, j)
                extra_chunks(i)

            x_round(0, 0)
            qv_round(0)
            with act.Fori(1, QV_LOOPS) as i:
                qv_round(i)
            qv_round(QV_LOOPS)

            act.wait_ge(s["angle_ready"], 1)
            act.activation(cos_sin[:, :], cos_sin[:, :], ACT.Sin).then_inc(s["cos_sin_ready"], 1)

            def m_round(sweep, g, slot, before, t):
                f_hi, v_hi = operands[:, 4 * slot, :], operands[:, 4 * slot + 2, :]
                act.wait_ge(s["m_summed"], freed(g, 2))
                act.copy(f_hi, tile_of(nodes, t))
                act.wait_ge(mv_loaded[slot], before * 16 + 16)
                act.activation(v_hi, stage[:, slot, :], ACT.Copy, scale=column(cos_sin, t * 2 + sweep))\
                    .then_inc(s["m_hi"], 1)

            def moments_hi(sweep):
                for b in range(B):
                    act.wait_ge(s["moment_ready"], 4 * sweep + b + 1)
                    act.copy(weights[:, 2 * sweep, b, :], stage[:, 2 + b, :]).then_inc(s["moment_hi"], 1)

            def m_rounds(sweep, loops, steps, seq0, span):
                with act.Fori(0, loops) as i:
                    for k in range(PER_TILE):
                        chunk(i + seq0, k)
                        if k == 3:
                            store_combined(i + (seq0 - 1))
                        for j in range(steps):
                            if k == j * span + span - 2:
                                n = 1 + j + sweep * TILES
                                m_round(sweep, i * steps + n, n % 2, i * (steps // 2) + n // 2, i * steps + (1 + j))
                    extra_chunks(i + seq0)
                moments_hi(sweep)

            act.wait_ge(s["cos_sin_ready"], 1)
            act.copy(cs_hi[:, :], cos_sin[:, :]).then_inc(s["cs_rounded"], 1)
            m_round(0, 0, 0, 0, 0)
            m_rounds(0, COS_LOOPS, COS_STEPS, COS_SEQ, 4)
            m_round(1, TILES, 1, TILES // 2, 0)
            m_rounds(1, SIN_LOOPS, SIN_STEPS, SIN_SEQ, 3)

            def o_round(n, slot):
                act.wait_ge(s["o_turned"], done(n))
                act.wait_ge(s["o_products"], freed(n, 2))
                act.copy(operands[:, 2 * slot, :], banks[1 + slot][:, :]).then_inc(s["o_hi"], 1)

            def o_first(n, slot):
                act.wait_ge(s["o_products"], done(n))
                act.wait_ge(s["o_norm_ready"], done(n))
                act.wait_ge(s["o_stats1"], freed(n, 1))
                act.activation(mix[:, :], banks[3 + 2 * slot][:, :], ACT.Copy,
                               scale=stats[:, 4 + slot, 4:5]).then_inc(s["o_first"], 1)

            def o_root(n, j, which):
                act.wait_ge(s[f"o_stats{which}"], done(n))
                act.activation(stats[:, j, 2:3], stats[:, j, 2:3], ACT.Sqrt).then_inc(s[f"o_root{which}"], 1)

            def o_last(n, j, r):
                z = stage[0:r, 2 + j, :]
                act.wait_ge(s["o_final"], done(n))
                act.activation(z, z, ACT.Identity, scale=stats[0:r, j, 3:4], bias=stats[0:r, j, 4:5])\
                    .then_inc(s["o_scaled2"], 1)
                act.wait_ge(s["o_scaled2"], done(n))
                act.dma_start(dram_rows(out, n, r), z).then_inc(o_stored[j], 16)

            def out_round(i):
                for k in range(PER_TILE):
                    if not isinstance(i, int) or i < OUT_LOOPS:
                        chunk(i + OUT_SEQ, k)
                    if k == 3:
                        store_combined(i + (OUT_SEQ - 1))
                    for n, j, at in in_flight(k, i, OUT_STEPS, 4):
                        if at == 3 and not after_last(n + 1):
                            o_round(n + 1, (j + 1) % 2)
                        if at == 6:
                            o_first(n, j % 2)
                        if at == 8:
                            o_root(n, j, 1)
                        if at == 11:
                            o_root(n, j, 2)
                        if at == 14:
                            o_last(n, j, TAIL if after_last(n + 1) else P)
                if not isinstance(i, int) or i < OUT_LOOPS:
                    extra_chunks(i + OUT_SEQ)

            o_round(0, 0)
            out_round(0)
            with act.Fori(1, OUT_LOOPS) as i:
                out_round(i)
            out_round(OUT_LOOPS)

        @block.vector
        def _(dve):
            def linked(name, item, count):
                step = [0]

                def link(ins, apart=False):
                    step[0] += 1
                    ins.then_inc(s[name], 1)
                    if apart:
                        wait_apart(dve, s[name], item * count + step[0])
                    else:
                        dve.wait_ge(s[name], item * count + step[0])
                return link

            link = linked("dve_chain", 0, 0)

            for name in ("g_x_split", "bins_ready", "chunk_split", "own_added", "gcn_combined", "qv_x_split",
                         "v_kept", "q_biased", "q_stats", "q_scaled", "m_split", "o_split", "o_norm_ready",
                         "o_stats1", "o_stats2", "o_final", "o_mixed", "chunk_hot"):
                dve.sem_inc(s[name], LEAD)
            extras_done = dve.alloc_register("dve_extras")
            dve.reg_mov(extras_done, 0)

            dve.wait_ge(s["consts_set"], 3)
            dve.wait_ge(s["dst_loaded"], 48)
            dve.wait_ge(s["src_loaded"], 48)
            dve.tensor_copy(dst_f, dst_nat).then_inc(s["edges_f"], 1)
            dve.tensor_copy(src_f, src_nat).then_inc(s["edges_f"], 1)
            dve.tensor_copy(ident_r[:, :], ident[:, :]).then_inc(s["ident_ready"], 1)
            dve.memset(plain(zeros_r[:, :]), 0.0).then_inc(s["ident_ready"], 1)
            dve.memset(row_sum[:, :], 0.0)
            dve.memset(ones[:, :], 1.0).then_inc(s["ident_ready"], 1)

            def split_weight(n, hi, lo):
                dve.wait_ge(s["raw_rounded"], n + 1)
                dve.tensor_tensor(lo, raws[n], plain(hi), ALU.subtract).then_inc(s["raw_split"], 1)

            split_weight(0, g_hi, g_lo)
            for g in range(2 * GROUPS):
                half = slice((g // 2) * P, (g // 2 + 1) * P)
                dve.wait_ge(s["edges_turned"], g + 1)
                dve.tensor_copy((src_cols if g % 2 else dst_cols)[:, half], banks[1 + g % 2][:, 0:P])\
                    .then_inc(s["edges_kept"], 1)
            dve.wait_ge(s["edges_kept"], 2 * GROUPS)
            link(dve.tensor_copy(dst_i, dst_cols[:, :]))
            link(dve.tensor_scalar(mod_i, dst_i, P - 1, None, ALU.bitwise_and))
            link(dve.tensor_scalar(div_i, dst_i, 7, None, ALU.arith_shift_right))
            link(dve.tensor_copy(dst_mod, mod_i))
            link(dve.tensor_copy(dst_div, div_i))
            nat = dst_f.rearrange("p (g e) -> p g e", e=P)
            link(dve.tensor_scalar(neg, dst_f, 0.0, 65536.0, ALU.is_lt, ALU.mult))
            link(dve.tensor_tensor(neg, neg, dst_f, ALU.add))
            link(dve.tensor_reduce(ext[:, 0:GROUPS], neg.rearrange("p (g e) -> p g e", e=P), AX.X, ALU.min))
            link(dve.tensor_reduce(ext[:, GROUPS:], nat, AX.X, ALU.max))
            wide = [P, TILES, GROUPS]
            across = lambda ap: ap.unsqueeze(1).to_broadcast(wide)
            down = lambda ap: ap.unsqueeze(2).to_broadcast(wide)
            link(dve.tensor_tensor(grid, across(ext[:, GROUPS:]), down(first_node[:, :]), ALU.is_ge))
            link(dve.tensor_scalar(small[:, 0:GROUPS], chunk_id, BIG, None, ALU.subtract))
            link(dve.tensor_tensor(grid, grid, across(small[:, 0:GROUPS]), ALU.mult))
            link(dve.tensor_reduce(lim_lo, grid, AX.X, ALU.min))
            link(dve.tensor_scalar(limit, first_node[:, :], float(P), None, ALU.add))
            link(dve.tensor_tensor(grid, across(ext[:, 0:GROUPS]), down(limit), ALU.is_lt))
            link(dve.tensor_scalar(small[:, 0:GROUPS], chunk_id, 1.0, None, ALU.add))
            link(dve.tensor_tensor(grid, grid, across(small[:, 0:GROUPS]), ALU.mult))
            dve.tensor_reduce(lim_hi, grid, AX.X, ALU.max).then_inc(s["limits_ready"], 1)
            dve.wait_ge(s["limits_turned"], 1)
            link(dve.tensor_reduce(col[0:TILES, 0:1], banks[1][0:TILES, 0:P], AX.X, ALU.min))
            link(dve.tensor_reduce(col[0:TILES, 1:2], banks[1][0:TILES, P:2 * P], AX.X, ALU.max))
            link(dve.tensor_scalar(col[0:TILES, 0:1], col[0:TILES, 0:1], BIG, float(CHUNKS - 1), ALU.add, ALU.min))
            link(dve.tensor_scalar(col[0:TILES, 2:3], col[0:TILES, 0:1], float(PER_TILE), None, ALU.add))
            dve.tensor_tensor(col[0:TILES, 1:2], col[0:TILES, 1:2], col[0:TILES, 2:3], ALU.max)\
                .then_inc(s["ranges_ready"], 1)
            dve.wait_ge(s["ranges_turned"], 1)
            dve.tensor_copy(schedule[:, :], banks[2][0:1, 0:2 * TILES]).then_inc(s["schedule_ready"], 1)
            dve.wait_ge(s["schedule_ready"], 1)
            dve.wait_ge(s["bias_loaded"], 48)
            dve.tensor_tensor(bias[:, 1, :], bias[:, 1, :], bias_raw, ALU.add).then_inc(s["setup_done"], 1)
            split_weight(1, weights[:, 0, :, :], weights[:, 1, :, :])
            split_weight(2, weights[:, 2, :, :], weights[:, 3, :, :])

            def bins(t, half):
                c0 = t * HIST + half * HALF[0]
                count = HALF[half]
                cols = lambda ap: (ap[:, c0:c0 + count] if isinstance(t, int) else ap[:, bass.ds(c0, count)])
                dve.wait_ge(s["bins_used"], freed(t * 2 + half, 2))
                dve.tensor_tensor(div_hot[half][:, 0:count, 0:TILES],
                                  iota_bf[:, 0:TILES].unsqueeze(1).to_broadcast([P, count, TILES]),
                                  cols(dst_div).unsqueeze(2).to_broadcast([P, count, TILES]), ALU.is_equal)
                dve.tensor_tensor(mod_hot[half][:, 0:count, :],
                                  iota_bf[:, :].unsqueeze(1).to_broadcast([P, count, P]),
                                  cols(dst_mod).unsqueeze(2).to_broadcast([P, count, P]), ALU.is_equal)\
                    .then_inc(s["bins_ready"], 1)

            def g_split(t, n, r):
                turned = banks[1 + n][:, :].rearrange("p (b c) -> p b c", c=P)[:, :, 0:r]
                x_hi = operands[:, n, :].rearrange("p (b c) -> p b c", c=P)[:, :, 0:r]
                x_lo = operands[:, 2 + n, :].rearrange("p (b c) -> p b c", c=P)[:, :, 0:r]
                dve.wait_ge(s["g_x_hi"], done(t))
                dve.tensor_tensor(x_lo, turned, plain(x_hi), ALU.subtract).then_inc(s["g_x_split"], 1)

            with dve.Fori(0, FULL // 2) as i:
                for n in range(2):
                    g_split(i * 2 + n, n, P)
                    bins(i * 2 + n, 0)
                    bins(i * 2 + n, 1)
            g_split(FULL, 0, P)
            bins(FULL, 0)
            bins(FULL, 1)

            dve.wait_ge(s["degrees_summed"], 1)
            dve.tensor_scalar(dinv[:, :], banks[5][:, 0:TILES], 1.0, 1e-12, ALU.add, ALU.max)\
                .then_inc(s["degrees_kept"], 1)
            dve.wait_ge(s["root_taken"], 1)
            dve.reciprocal(dinv[:, :], dinv[:, :]).then_inc(s["dinv_ready"], 1)
            dve.wait_ge(s["dinv_ready"], 1)
            dve.wait_ge(s["g_kept"], done(FULL))
            with dve.Fori(0, FULL // 4) as i:
                for n in range(4):
                    g = tile_of(nodes, i * 4 + n)
                    dve.tensor_scalar(g, g, column(dinv, i * 4 + n), None, ALU.mult).then_inc(s["g_scaled"], 1)
            g = tile_of(nodes, FULL)
            dve.tensor_scalar(g, g, dinv[:, FULL:FULL + 1], None, ALU.mult).then_inc(s["g_scaled"], 1)

            def begin_tile(seq):
                first = dve.value_load(column(schedule, seq), min_val=0, max_val=CHUNKS - 1)
                dve.wait_ge(s["chunk_hot"], freed(chunk_number(seq, 0), 1))
                dve.tensor_scalar(tile_id[:, :], node_id[:, :], column(first_node, seq), None, ALU.add)\
                    .then_inc(s["tile_id_ready"], 1)
                dve.wait_ge(s["tile_id_ready"], seq + 1)
                return first

            def chunk(seq, k, first):
                n = chunk_number(seq, k)
                dve.wait_ge(s["chunk_summed"], freed(n, SPLIT))
                dve.tensor_scalar(one_hot[:, k % SPLIT, :], tile_id[:, :], column(dst_cols, first + k), None,
                                  ALU.is_equal).then_inc(s["chunk_hot"], 1)
                dve.wait_ge(s["chunk_rounded"], done(n))
                dve.tensor_tensor(row_ring[k % RING], plain(row_ring[k % RING]), plain(hi_ring[k % SPLIT]), ALU.subtract)\
                    .then_inc(s["chunk_split"], 1)

            def add_own(seq):
                dve.wait_ge(s["combine_loaded"], seq * 16 + 16)
                dve.wait_ge(s["own_loaded"], seq * 16 + 16)
                dve.scalar_tensor_tensor(combine[:, :], own_rows[:, :], column(dinv, seq), combine[:, :],
                                         ALU.mult, ALU.add).then_inc(s["own_added"], 1)

            def extra_chunks(seq, first):
                end = dve.value_load(column(schedule, seq + TILES), min_val=PER_TILE, max_val=CHUNKS - 1 + PER_TILE)
                with dve.If(end > first + PER_TILE):
                    wait_apart(dve, s["chunk_summed"], done(chunk_number(seq, PER_TILE - 1)))
                    with dve.Fori(first + PER_TILE, end) as c:
                        had = dve.snap(extras_done)
                        dve.tensor_scalar(one_hot[:, 0, :], tile_id[:, :], column(dst_cols, c),
                                          None, ALU.is_equal)
                        dve.wait_ge(s["extra_rounded"], had + 1)
                        dve.tensor_tensor(row_ring[0], plain(row_ring[0]), plain(hi_ring[0]), ALU.subtract)\
                            .then_inc(s["extra_split"], 1)
                        dve.wait_ge(s["extra_summed"], had + 1)
                        dve.reg_add(extras_done, extras_done, 1)

            def combine_tile(seq):
                if exists(seq):
                    dve.wait_ge(s["own_added"], done(seq))
                    dve.wait_ge(s["gcn_summed"], done(seq))
                    dve.scalar_tensor_tensor(combine[:, :], gcn_bank[:, :], column(dinv, seq), combine[:, :],
                                             ALU.mult, ALU.add).then_inc(s["gcn_combined"], 1)

            def chunk_step(seq, k, first):
                chunk(seq, k, first)
                if k == 1:
                    combine_tile(seq - 1)
                if k == 16:
                    add_own(seq)

            def x_split(t, j):
                dve.wait_ge(s["qv_x_hi"], done(t))
                dve.tensor_tensor(operands[:, 3 + j, :], banks[1][:, :], plain(operands[:, j, :]), ALU.subtract)\
                    .then_inc(s["qv_x_split"], 1)

            def v_keep(stores, t, j):
                dve.wait_ge(v_stored[j], stores * 16)
                dve.wait_ge(s["v_summed"], done(t))
                dve.tensor_tensor(stage[:, 3 + j, :], banks[2 + j][:, :], bias[:, 1, :], ALU.add)\
                    .then_inc(s["v_kept"], 1)

            def q_bias(t, j):
                dve.wait_ge(s["q_summed"], done(t))
                dve.tensor_tensor(tile_of(nodes, t), banks[5 + j][:, :], bias[:, 0, :], ALU.add)\
                    .then_inc(s["q_biased"], 1)

            def q_variance(t, j):
                link = linked("variance_linked", t, 2)
                wait_apart(dve, s["q_rect"], done(t))
                link(dve.bn_stats(bn_parts[:, j, :], tile_of(nodes, t)), True)
                link(dve.bn_aggr(stats[:, j, 0:2], bn_parts[:, j, :]))
                dve.tensor_scalar(stats[:, j, 2:3], stats[:, j, 1:2], LN_EPS, None, ALU.add)\
                    .then_inc(s["q_stats"], 1)

            def q_factors(t, j):
                link = linked("factors_linked", t, 1)
                dve.wait_ge(s["q_root"], done(t))
                link(dve.reciprocal(stats[:, j, 3:4], stats[:, j, 2:3]))
                dve.scalar_tensor_tensor(stats[:, j, 4:5], stats[:, j, 0:1], -1.0, stats[:, j, 3:4],
                                         ALU.mult, ALU.mult).then_inc(s["q_scaled"], 1)

            def qv_round(i):
                first = begin_tile(i)
                for k in range(PER_TILE):
                    chunk_step(i, k, first)
                    for t, j, at in in_flight(k, i, QV_STEPS, 6):
                        if at == 4:
                            v_keep(i, t, j)
                        if at == 5 and not after_last(t + 1):
                            x_split(t + 1, (j + 1) % QV_STEPS)
                        if at == 7:
                            q_bias(t, j)
                        if at == 10:
                            q_variance(t, j)
                        if at == 13:
                            q_factors(t, j)
                extra_chunks(i, first)

            x_split(0, 0)
            qv_round(0)
            with dve.Fori(1, QV_LOOPS) as i:
                qv_round(i)
            qv_round(QV_LOOPS)

            dve.wait_ge(s["q_kept"], done(FULL))
            h = stage[:, 2, 0:TILES]
            turns = stage[:, 2, 64:64 + TILES]
            link(dve.tensor_tensor(h, row_sum[:, :], row_sum[:, :], ALU.mult))
            for n, op in enumerate((ALU.max, ALU.min)):
                link(dve.tensor_reduce(small[:, n:n + 1], h[:, 0:FULL], AX.X, op))
                link(dve.tensor_tensor(small[0:TAIL, n:n + 1], small[0:TAIL, n:n + 1], h[0:TAIL, FULL:TILES], op))
            dve.tensor_scalar(small[:, 1:2], small[:, 1:2], -1.0, None, ALU.mult).then_inc(s["spread_step"], 1)
            dve.wait_ge(s["extremes_turned"], 1)
            link(dve.tensor_reduce(small[0:1, 2:3], banks[1][0:1, 0:P], AX.X, ALU.max))
            link(dve.tensor_reduce(small[0:1, 3:4], banks[1][0:1, P:2 * P], AX.X, ALU.max))
            link(dve.tensor_tensor(small[0:1, 4:5], small[0:1, 2:3], small[0:1, 3:4], ALU.add))
            link(dve.tensor_scalar(small[0:1, 4:5], small[0:1, 4:5], 4.0, None, ALU.mult))
            link(dve.reciprocal(small[0:1, 5:6], small[0:1, 4:5]))
            dve.tensor_scalar(small[0:1, 6:7], small[0:1, 5:6], PI, None, ALU.mult).then_inc(s["spread_step"], 1)
            dve.wait_ge(s["factor_spread"], 1)
            link(dve.tensor_copy(small[:, 7:8], banks[2][:, 0:1]))
            link(dve.tensor_scalar(h, h, small[:, 7:8], None, ALU.mult))
            link(dve.tensor_scalar(turns, h, 1.0 / (2 * PI), ROUND, ALU.mult, ALU.add))
            link(dve.tensor_scalar(turns, turns, ROUND, None, ALU.subtract))
            for turn in (TURN_HI, TURN_MID, TURN_LO):
                link(dve.scalar_tensor_tensor(h, turns, -turn, h, ALU.mult, ALU.add))
            link(dve.tensor_scalar(h, h, 3.1415925, -3.1415925, ALU.min, ALU.max))
            pair = cos_sin[:, :].rearrange("p (t c) -> p t c", c=2)
            link(dve.tensor_copy(pair[:, :, 1], h))
            link(dve.scalar_tensor_tensor(turns, h, -1.0, h, ALU.mult, ALU.max))
            dve.tensor_scalar(pair[:, :, 0], turns, -1.0, HALF_PI, ALU.mult, ALU.add).then_inc(s["angle_ready"], 1)
            dve.wait_ge(s["cs_rounded"], 1)
            dve.tensor_tensor(cs_lo[:, :], cos_sin[:, :], plain(cs_hi[:, :]), ALU.subtract)\
                .then_inc(s["cs_split"], 1)

            def m_split(sweep, g, slot, t):
                f_hi, f_lo = operands[:, 4 * slot, :], operands[:, 4 * slot + 1, :]
                v_hi, v_lo = operands[:, 4 * slot + 2, :], operands[:, 4 * slot + 3, :]
                dve.wait_ge(s["m_hi"], done(g))
                dve.tensor_tensor(f_lo, tile_of(nodes, t), plain(f_hi), ALU.subtract)
                dve.scalar_tensor_tensor(v_lo, stage[:, slot, :], column(cos_sin, t * 2 + sweep),
                                         plain(v_hi), ALU.mult, ALU.subtract).then_inc(s["m_split"], 1)

            def moments(sweep):
                dve.wait_ge(s["m_summed"], done(sweep * TILES + FULL))
                dve.wait_ge(s["rows_bias_loaded"], 32)
                if sweep == 0:
                    link(dve.tensor_copy(moment_sums[:, :], banks[7][:, 0:8]))
                    link(dve.tensor_copy(sums_hi[:, :], moment_sums[:, :]))
                    link(dve.tensor_tensor(sums_lo[:, :], moment_sums[:, :], plain(sums_hi[:, :]), ALU.subtract))
                    link(dve.tensor_scalar(moment_sums[:, :], moment_sums[:, :], -1.0, None, ALU.mult))
                else:
                    dve.wait_ge(s["moment_split"], 4)
                for b in range(B):
                    at = 2 * b + sweep
                    dve.scalar_tensor_tensor(stage[:, 2 + b, :], bias[:, 1, :], moment_sums[:, at:at + 1],
                                             banks[3 + b][:, :], ALU.mult, ALU.add).then_inc(s["moment_ready"], 1)
                for b in range(B):
                    dve.wait_ge(s["moment_hi"], 4 * sweep + b + 1)
                    dve.tensor_tensor(weights[:, 2 * sweep + 1, b, :], stage[:, 2 + b, :],
                                      plain(weights[:, 2 * sweep, b, :]), ALU.subtract)\
                        .then_inc(s["moment_split"], 1)

            def m_rounds(sweep, loops, steps, seq0, span):
                with dve.Fori(0, loops) as i:
                    first = begin_tile(i + seq0)
                    for k in range(PER_TILE):
                        chunk_step(i + seq0, k, first)
                        for j in range(steps):
                            if k == j * span + span - 2:
                                n = 1 + j + sweep * TILES
                                m_split(sweep, i * steps + n, n % 2, i * steps + (1 + j))
                    extra_chunks(i + seq0, first)
                moments(sweep)

            m_split(0, 0, 0, 0)
            m_rounds(0, COS_LOOPS, COS_STEPS, COS_SEQ, 4)
            m_split(1, TILES, 1, 0)
            m_rounds(1, SIN_LOOPS, SIN_STEPS, SIN_SEQ, 3)

            def o_split(n, slot):
                dve.wait_ge(s["o_hi"], done(n))
                dve.tensor_tensor(operands[:, 2 * slot + 1, :], banks[1 + slot][:, :],
                                  plain(operands[:, 2 * slot, :]), ALU.subtract).then_inc(s["o_split"], 1)

            def o_norm(n, slot):
                st = stats[:, 4 + slot, :]
                both = banks[7][:, 0:2]
                c, sn = column(cos_sin, n * 2), column(cos_sin, n * 2 + 1)
                link = linked("norm_linked", n, 5)
                dve.wait_ge(s["o_normed"], done(n))
                link(dve.tensor_scalar(st[:, 0:1], both[:, 0:1], c, None, ALU.mult))
                link(dve.scalar_tensor_tensor(st[:, 1:2], both[:, 1:2], sn, st[:, 0:1], ALU.mult, ALU.add))
                link(dve.tensor_scalar(st[:, 2:3], st[:, 1:2], NORM_EPS, None, ALU.add))
                link(dve.reciprocal(st[:, 3:4], st[:, 2:3]))
                link(dve.tensor_scalar(st[:, 4:5], c, st[:, 3:4], None, ALU.mult))
                dve.tensor_scalar(st[:, 5:6], sn, st[:, 3:4], None, ALU.mult).then_inc(s["o_norm_ready"], 1)

            def mean_variance(link, j, data):
                link(dve.bn_stats(bn_parts[:, 0, :], data), True)
                link(dve.bn_aggr(stats[:, j, 0:2], bn_parts[:, 0, :]))
                return dve.tensor_scalar(stats[:, j, 2:3], stats[:, j, 1:2], LN_EPS, None, ALU.add)

            def o_mix(i, n, j):
                u, z, slot = mix[:, :], stage[:, 2 + j, :], j % 2
                link = linked("mix_linked", n, 3)
                dve.wait_ge(s["o_first"], done(n))
                dve.scalar_tensor_tensor(u, banks[4 + 2 * slot][:, :], stats[:, 4 + slot, 5:6], u,
                                         ALU.mult, ALU.add).then_inc(s["o_mixed"], 1)
                dve.wait_ge(s["o_mixed"], done(n))
                dve.wait_ge(oc_loaded[j], i * 16 + 16)
                link(dve.tensor_tensor(z, z, u, ALU.add), True)
                mean_variance(link, j, z).then_inc(s["o_stats1"], 1)

            def o_affine(i, n, j):
                z, st = stage[:, 2 + j, :], stats[:, j, :]
                link = linked("affine_linked", n, 6)
                dve.wait_ge(s["o_root1"], done(n))
                link(dve.reciprocal(st[:, 3:4], st[:, 2:3]))
                link(dve.scalar_tensor_tensor(z, z, st[:, 0:1], bias[:, 0, :], ALU.subtract, ALU.mult))
                link(dve.scalar_tensor_tensor(z, z, st[:, 3:4], bias[:, 1, :], ALU.mult, ALU.add))
                dve.wait_ge(ox_loaded[j % 2], i * 32 + (j // 2 * 16 + 16))
                link(dve.scalar_tensor_tensor(z, z, 0.0, stage[:, j % 2, :], ALU.max, ALU.add), True)
                mean_variance(link, j, z).then_inc(s["o_stats2"], 1)

            def o_factors(n, j):
                st = stats[:, j, :]
                link = linked("o_factors_linked", n, 1)
                dve.wait_ge(s["o_root2"], done(n))
                link(dve.reciprocal(st[:, 3:4], st[:, 2:3]))
                dve.scalar_tensor_tensor(st[:, 4:5], st[:, 0:1], -1.0, st[:, 3:4], ALU.mult, ALU.mult)\
                    .then_inc(s["o_final"], 1)

            def out_round(i):
                summing = not isinstance(i, int) or i < OUT_LOOPS
                first = begin_tile(i + OUT_SEQ) if summing else None
                if not summing:
                    combine_tile(i + (OUT_SEQ - 1))
                for k in range(PER_TILE):
                    if summing:
                        chunk_step(i + OUT_SEQ, k, first)
                    for n, j, at in in_flight(k, i, OUT_STEPS, 4):
                        if at == 3 and not after_last(n + 1):
                            o_split(n + 1, (j + 1) % 2)
                        if at == 3:
                            o_norm(n, j % 2)
                        if at == 6:
                            o_mix(i if at <= k else i - 1, n, j)
                        if at == 9:
                            o_affine(i if at <= k else i - 1, n, j)
                        if at == 12:
                            o_factors(n, j)
                if summing:
                    extra_chunks(i + OUT_SEQ, first)

            dve.wait_ge(s["rows_bias_loaded"], 48)
            o_split(0, 0)
            out_round(0)
            with dve.Fori(1, OUT_LOOPS) as i:
                out_round(i)
            out_round(OUT_LOOPS)

        @block.tensor
        def _(pe):
            for name in ("g_x_turned", "g_summed", "bins_used", "chunk_summed", "gcn_summed", "qv_x_turned",
                         "v_summed", "q_summed", "m_summed", "o_turned", "o_normed", "o_products"):
                pe.sem_inc(s[name], LEAD)
            extras_done = pe.alloc_register("pe_extras")
            pe.reg_mov(extras_done, 0)

            def products(out_ap, pairs, start, stop):
                for n, ((a_hi, a_lo), (b_hi, b_lo)) in enumerate(pairs):
                    pe.matmul(out_ap, a_hi, b_hi, start=start and n == 0, stop=False, skip_group_check=True)
                    pe.matmul(out_ap, a_hi, b_lo, start=False, stop=False, skip_group_check=True)
                    last = pe.matmul(out_ap, a_lo, b_hi, start=False, stop=stop and n == len(pairs) - 1,
                                     skip_group_check=True)
                return last

            pe.wait_ge(s["consts_set"], 3)
            pe.wait_ge(s["edges_f"], 2)
            for g in range(2 * GROUPS):
                if g >= 2:
                    pe.wait_ge(s["edges_kept"], g - 1)
                source = src_f if g % 2 else dst_f
                pe.transpose(banks[1 + g % 2][:, 0:P], source[:, (g // 2) * P:(g // 2 + 1) * P], ident[:, :])\
                    .then_inc(s["edges_turned"], 1)
            pe.wait_ge(s["limits_ready"], 1)
            pe.matmul(banks[1][0:TILES, 0:P], lim_lo, ident[:, :], start=True, stop=True)
            pe.matmul(banks[1][0:TILES, P:2 * P], lim_hi, ident[:, :], start=True, stop=True)\
                .then_inc(s["limits_turned"], 1)
            pe.wait_ge(s["ranges_ready"], 1)
            pe.matmul(banks[2][0:1, 0:TILES], col[0:TILES, 0:1], ident[0:TILES, 0:TILES], start=True, stop=True)
            pe.matmul(banks[2][0:1, TILES:2 * TILES], col[0:TILES, 1:2], ident[0:TILES, 0:TILES],
                      start=True, stop=True).then_inc(s["ranges_turned"], 1)
            pe.wait_ge(s["setup_done"], 1)
            pe.wait_ge(s["ident_ready"], 3)

            def turn(bank_, x_in, r):
                for b in range(B):
                    last = pe.transpose(bank_[:, b * P:b * P + r], x_in[0:r, b * P:(b + 1) * P], ident[0:r, 0:r])
                return last

            def g_turn(t, i, n, r):
                pe.wait_ge(g_x_loaded[n], i * 16 + 16)
                pe.wait_ge(s["g_x_split"], freed(t, 2))
                turn(banks[1 + n], stage[:, n, :], r).then_inc(s["g_x_turned"], 1)

            def bins(t, half):
                pe.wait_ge(s["bins_ready"], done(t * 2 + half))
                for c in range(HALF[half]):
                    last = pe.matmul(banks[5][:, 0:TILES], mod_hot[half][:, c, :], div_hot[half][:, c, 0:TILES],
                                     start=False, stop=False, skip_group_check=True)
                last.then_inc(s["bins_used"], 1)

            def g_product(t, n, r):
                pe.wait_ge(s["g_x_split"], done(t))
                pe.wait_ge(s["g_kept"], freed(t, 2))
                pairs = [((operands[:, n, b * P:b * P + r], operands[:, 2 + n, b * P:b * P + r]),
                          (g_hi[:, b, :], g_lo[:, b, :])) for b in range(B)]
                products(banks[3 + n][0:r, :], pairs, True, True).then_inc(s["g_summed"], 1)

            pe.wait_ge(s["raw_split"], 1)
            pe.matmul(banks[5][:, 0:TILES], zero_bf[:, :], zero_bf[:, 0:TILES], start=True, stop=False,
                      skip_group_check=True)
            with pe.Fori(0, FULL // 2) as i:
                g_turn(i * 2, i, 0, P)
                g_turn(i * 2 + 1, i, 1, P)
                for n in range(2):
                    g_product(i * 2 + n, n, P)
                    bins(i * 2 + n, 0)
                    bins(i * 2 + n, 1)
            g_turn(FULL, FULL // 2, 0, P)
            g_product(FULL, 0, P)
            bins(FULL, 0)
            bins(FULL, 1)
            pe.matmul(banks[5][:, 0:TILES], zero_bf[:, :], zero_bf[:, 0:TILES], start=False, stop=True,
                      skip_group_check=True).then_inc(s["degrees_summed"], 1)

            def chunk(seq, k):
                slot = k % SPLIT
                if k == 0:
                    pe.wait_ge(s["gcn_combined"], freed(seq, 1))
                pe.wait_ge(s["chunk_split"], done(chunk_number(seq, k)))
                pe.matmul(gcn_bank[:, :], one_hot[:, slot, :], hi_ring[slot], start=k == 0, stop=False,
                          skip_group_check=True)
                pe.matmul(gcn_bank[:, :], one_hot[:, slot, :], row_ring[k % RING], start=False, stop=False,
                          skip_group_check=True).then_inc(s["chunk_summed"], 1)

            def end_tile(seq):
                first = pe.value_load(column(schedule, seq), min_val=0, max_val=CHUNKS - 1)
                end = pe.value_load(column(schedule, seq + TILES), min_val=PER_TILE, max_val=CHUNKS - 1 + PER_TILE)
                with pe.If(end > first + PER_TILE):
                    with pe.Fori(first + PER_TILE, end):
                        had = pe.snap(extras_done)
                        pe.wait_ge(s["extra_split"], had + 1)
                        pe.matmul(gcn_bank[:, :], one_hot[:, 0, :], hi_ring[0], start=False, stop=False,
                                  skip_group_check=True)
                        pe.matmul(gcn_bank[:, :], one_hot[:, 0, :], row_ring[0], start=False, stop=False,
                                  skip_group_check=True).then_inc(s["extra_summed"], 1)
                        pe.reg_add(extras_done, extras_done, 1)
                pe.matmul(gcn_bank[:, 0:8], ident_r[:, :], zeros_r[:, 0:8], start=False, stop=True,
                          skip_group_check=True).then_inc(s["gcn_summed"], 1)

            def x_turn(t, before, j):
                pe.wait_ge(x_loaded[j], before * 16 + 16)
                pe.wait_ge(s["qv_x_split"], freed(t, 1))
                turn(banks[1], stage[:, j, :], P).then_inc(s["qv_x_turned"], 1)

            def x_product(bank_, j, blocks, which):
                pairs = [((operands[:, j, b * P:(b + 1) * P], operands[:, 3 + j, b * P:(b + 1) * P]),
                          (weights[:, which, b, :], weights[:, which + 1, b, :])) for b in blocks]
                return products(bank_[:, :], pairs, blocks[0] == 0, blocks[-1] == B - 1)

            def qv_round(i, steps):
                for k in range(PER_TILE):
                    for j in range(steps):
                        t, at = i * QV_STEPS + j, k - 6 * j
                        if at == 0:
                            pe.wait_ge(s["qv_x_split"], done(t))
                            pe.wait_ge(s["v_kept"], freed(t, QV_STEPS))
                            pe.wait_ge(s["q_biased"], freed(t, QV_STEPS))
                            x_product(banks[2 + j], j, [0, 1], 2)
                        if at == 1:
                            x_product(banks[2 + j], j, [2, 3], 2).then_inc(s["v_summed"], 1)
                        if at == 2:
                            if steps > 1:
                                x_turn(t + 1, i + (j + 1) // QV_STEPS, (j + 1) % QV_STEPS)
                            x_product(banks[5 + j], j, [0, 1], 0)
                        if at == 3:
                            x_product(banks[5 + j], j, [2], 0)
                        if at == 4:
                            x_product(banks[5 + j], j, [3], 0).then_inc(s["q_summed"], 1)
                    chunk(i, k)
                end_tile(i)

            pe.wait_ge(s["raw_split"], 3)
            x_turn(0, 0, 0)
            with pe.Fori(0, QV_LOOPS) as i:
                qv_round(i, QV_STEPS)
            qv_round(QV_LOOPS, 1)

            pe.wait_ge(s["spread_step"], 1)
            pe.matmul(banks[1][0:1, 0:P], small[:, 0:1], ident[:, :], start=True, stop=True)
            pe.matmul(banks[1][0:1, P:2 * P], small[:, 1:2], ident[:, :], start=True, stop=True)\
                .then_inc(s["extremes_turned"], 1)
            pe.wait_ge(s["spread_step"], 2)
            pe.matmul(banks[2][:, 0:1], ones[:, :], small[0:1, 6:7], start=True, stop=True)\
                .then_inc(s["factor_spread"], 1)

            def m_products(sweep, slot, t, r, blocks):
                f = operands[0:r, 4 * slot, :], operands[0:r, 4 * slot + 1, :]
                v = operands[0:r, 4 * slot + 2, :], operands[0:r, 4 * slot + 3, :]
                pairs_cs = [ap[0:r, 2 * t:2 * t + 2] if isinstance(t, int) else ap[0:r, bass.ds(t * 2, 2)]
                            for ap in (cs_hi, cs_lo)]
                for b in blocks:
                    f_b = f[0][:, b * P:(b + 1) * P], f[1][:, b * P:(b + 1) * P]
                    last = products(banks[3 + b][:, :], [(f_b, v)], False, False)
                    if sweep == 0:
                        last = products(banks[7][:, 2 * b:2 * b + 2], [(f_b, pairs_cs)], False, False)
                return last

            def m_rounds(sweep, loops, steps, seq0, span):
                pe.wait_ge(s["m_split"], done(sweep * TILES))
                for b in range(B):
                    pe.matmul(banks[3 + b][:, :], zeros_r[:, :], operands[:, 4 * sweep + 2, :],
                              start=True, stop=False, skip_group_check=True)
                with pe.Fori(0, loops) as i:
                    for k in range(PER_TILE):
                        for j in range(steps):
                            at = k - span * j
                            if at == 0:
                                pe.wait_ge(s["m_split"], done(i * steps + (j + sweep * TILES)))
                            if 0 <= at < span:
                                blocks = [at] if span == 4 else ([0, 1], [2], [3])[at]
                                last = m_products(sweep, (j + sweep) % 2, i * steps + j, P, blocks)
                                if at == span - 1:
                                    last.then_inc(s["m_summed"], 1)
                        chunk(i + seq0, k)
                    end_tile(i + seq0)
                pe.wait_ge(s["m_split"], done(FULL + sweep * TILES))
                m_products(sweep, sweep, FULL, TAIL, range(B)).then_inc(s["m_summed"], 1)

            pe.wait_ge(s["v_kept"], done(FULL))
            pe.wait_ge(s["q_biased"], done(FULL))
            pe.wait_ge(s["cs_split"], 1)
            pe.matmul(banks[7][:, 0:8], zeros_r[:, :], zeros_r[:, 0:8], start=True, stop=False, skip_group_check=True)
            m_rounds(0, COS_LOOPS, COS_STEPS, COS_SEQ, 4)
            pe.wait_ge(s["moment_ready"], 4)
            m_rounds(1, SIN_LOOPS, SIN_STEPS, SIN_SEQ, 3)

            def o_turn(n, before, slot):
                pe.wait_ge(oq_loaded[slot], before * 16 + 16)
                pe.wait_ge(s["o_split"], freed(n, 2))
                turn(banks[1 + slot], plain(operands[:, 4 + slot, :]), P).then_inc(s["o_turned"], 1)

            def o_pairs(slot, blocks):
                hi, lo = operands[:, 2 * slot, :], operands[:, 2 * slot + 1, :]
                return [(hi[:, b * P:(b + 1) * P], lo[:, b * P:(b + 1) * P]) for b in blocks]

            def o_norms(n, slot):
                pe.wait_ge(s["o_norm_ready"], freed(n, 1))
                pairs = [(f, (sums_hi[:, 2 * b:2 * b + 2], sums_lo[:, 2 * b:2 * b + 2]))
                         for b, f in enumerate(o_pairs(slot, range(B)))]
                products(banks[7][:, 0:2], pairs, True, True).then_inc(s["o_normed"], 1)

            def o_product(which, slot, blocks):
                pairs = [(f, (weights[:, 2 * which, b, :], weights[:, 2 * which + 1, b, :]))
                         for b, f in zip(blocks, o_pairs(slot, blocks))]
                return products(banks[3 + 2 * slot + which][:, :], pairs, blocks[0] == 0, blocks[-1] == B - 1)

            def out_round(i, steps):
                for k in range(PER_TILE if steps > 1 else 4):
                    for j in range(steps):
                        n, at, slot = i * OUT_STEPS + j, k - 4 * j, j % 2
                        if at == 0:
                            if steps > 1:
                                o_turn(n + 1, i * 2 + (j + 1) // 2, (j + 1) % 2)
                            pe.wait_ge(s["o_split"], done(n))
                            pe.wait_ge(s["o_mixed"], freed(n, 2))
                            o_norms(n, slot)
                            o_product(0, slot, [0, 1])
                        if at == 1:
                            o_product(0, slot, [2, 3])
                        if at == 2:
                            o_product(1, slot, [0, 1])
                        if at == 3:
                            o_product(1, slot, [2, 3]).then_inc(s["o_products"], 1)
                    if steps > 1:
                        chunk(i + OUT_SEQ, k)
                if steps > 1:
                    end_tile(i + OUT_SEQ)

            pe.wait_ge(s["moment_split"], 8)
            o_turn(0, 0, 0)
            with pe.Fori(0, OUT_LOOPS) as i:
                out_round(i, OUT_STEPS)
            out_round(OUT_LOOPS, 1)


_INS = ["x", "src", "dst", "L0_gnn_Wq", "L0_gnn_bq", "L0_gnn_Wv", "L0_gnn_bv", "L0_gnn_Wg", "L0_gnn_bg",
        "L0_gnn_gamma", "L0_gnn_beta"]


def kernel(**inputs):
    import concourse.bacc as bacc
    from concourse.bass_utils import run_bass_kernel_spmd

    nc = bacc.Bacc("TRN2", target_bir_lowering=False, num_devices=1)
    arrays, args = {}, []
    for name in _INS:
        a = np.ascontiguousarray(inputs[name])
        arrays[f"in_{name}"] = a
        args.append(nc.dram_tensor(f"in_{name}", a.shape, mybir.dt.from_np(a.dtype), kind="ExternalInput").ap())
    out = nc.dram_tensor("out", inputs["x"].shape, F32, kind="ExternalOutput").ap()
    build_layer(nc, *args, out)
    r = run_bass_kernel_spmd(nc, [arrays], core_ids=[0])
    return r.results[0]["out"]
```
